# Optimizing a Trainium2 kernel written in Bass

```python
import numpy as np
import jax
import jax.numpy as jnp

def _softmax(x, axis=-1):
    return jax.nn.softmax(x, axis=axis)
def _gelu(x):
    return jax.nn.gelu(x, approximate=True)
def _silu(x):
    return jax.nn.silu(x)
def _sigmoid(x):
    return jax.nn.sigmoid(x)
def _layernorm(x, axis=-1, eps=1e-5):
    m = jnp.mean(x, axis=axis, keepdims=True)
    v = jnp.var(x, axis=axis, keepdims=True)
    return (x - m) / jnp.sqrt(v + eps)
def _scatter_add(tgt, idx, src, axis=0):
    return tgt.at[idx].add(src)
def _segment_sum(src, seg, n):
    return jax.ops.segment_sum(src, seg, n)

kernel_name = 'mk_adj_ffn_d1_adj_256_90e4c5'

def setup_inputs(seed: int = 0):
    np.random.seed(seed)
    _w = jnp.asarray
    def _rec_inputs():
        import jax
        import jax.numpy as jnp
        _gk = jax.random.key(seed)
        x = -0.0005207 + 1.001 * jax.random.normal(jax.random.fold_in(_gk, 1), (4096, 256), jnp.float32)
        _a = jax.random.bernoulli(jax.random.fold_in(_gk, 2), 0.00390625, (4096, 4096))
        _a = jnp.logical_or(_a, jnp.swapaxes(_a, -1, -2))
        _a = jnp.logical_or(_a, jnp.eye(4096, dtype=bool))
        _af = _a.astype(jnp.float32)
        adj = _af
        return x, adj
    x, adj = _rec_inputs()
    def _L0_gnn_setup():
        import jax, jax.numpy as jnp
        import numpy as np
        NEG_INF = -9000000000000000.0
        NEG_SLOPE = 0.2
        key = jax.random.key(seed)
        k1, k2, k3, k4 = jax.random.split(key, 4)
        N, d_in, d_out = (8192, 256, 256)
        x = jax.random.normal(k1, (N, d_in), dtype=jnp.float32)
        adj = jax.random.randint(k2, (N, N), 0, 2).astype(jnp.float32)
        W = jax.random.normal(k3, (d_in, d_out), dtype=jnp.float32) * (1.0 / np.sqrt(d_in))
        a = jax.random.normal(k4, (2 * d_out,), dtype=jnp.float32) * (1.0 / np.sqrt(2 * d_out))
        return {'x': x, 'adj': adj, 'W': W, 'a': a}
    _L0_gnn_all = _L0_gnn_setup()
    _L0_gnn_in = {k: v for k, v in _L0_gnn_all.items() if k in ('W', 'a', )}
    del _L0_gnn_all

    def _L0_ffn_setup():
        import jax, jax.numpy as jnp
        import numpy as np
        TOP_K = 2
        LN_EPS = 1e-05
        key = jax.random.key(seed)
        ks = jax.random.split(key, 8)
        B, S, D, E, H = (16, 1024, 256, 8, 1024)
        x = jax.random.normal(ks[0], (B, S, D), dtype=jnp.float32)
        Wr = jax.random.normal(ks[1], (D, E), dtype=jnp.float32) * 0.1
        br = jnp.zeros((E,), dtype=jnp.float32)
        ln_g = jnp.ones((E, D), dtype=jnp.float32)
        ln_b = jnp.zeros((E, D), dtype=jnp.float32)
        W1 = jax.random.normal(ks[2], (E, D, H), dtype=jnp.float32) * (1.0 / np.sqrt(D))
        b1 = jnp.zeros((E, H), dtype=jnp.float32)
        W2 = jax.random.normal(ks[3], (E, H, D), dtype=jnp.float32) * (1.0 / np.sqrt(H))
        b2 = jnp.zeros((E, D), dtype=jnp.float32)
        return {'x': x, 'Wr': Wr, 'br': br, 'ln_g': ln_g, 'ln_b': ln_b, 'W1': W1, 'b1': b1, 'W2': W2, 'b2': b2}
    _L0_ffn_all = _L0_ffn_setup()
    _L0_ffn_in = {k: v for k, v in _L0_ffn_all.items() if k in ('Wr', 'br', 'ln_g', 'ln_b', 'W1', 'b1', 'W2', 'b2', )}
    del _L0_ffn_all

    return {
        "x": x,
        "adj": adj,
        "L0_gnn_W": _L0_gnn_in["W"],
        "L0_gnn_a": _L0_gnn_in["a"],
        "L0_ffn_Wr": _L0_ffn_in["Wr"],
        "L0_ffn_br": _L0_ffn_in["br"],
        "L0_ffn_ln_g": _L0_ffn_in["ln_g"],
        "L0_ffn_ln_b": _L0_ffn_in["ln_b"],
        "L0_ffn_W1": _L0_ffn_in["W1"],
        "L0_ffn_b1": _L0_ffn_in["b1"],
        "L0_ffn_W2": _L0_ffn_in["W2"],
        "L0_ffn_b2": _L0_ffn_in["b2"],
    }

def reference(x, adj, L0_gnn_W, L0_gnn_a, L0_ffn_Wr, L0_ffn_br, L0_ffn_ln_g, L0_ffn_ln_b, L0_ffn_W1, L0_ffn_b1, L0_ffn_W2, L0_ffn_b2):
    import jax
    import jax.numpy as jnp
    def _L0_gnn_ref(x, adj, W, a):
        import jax, jax.numpy as jnp
        import numpy as np
        NEG_INF = -9000000000000000.0
        NEG_SLOPE = 0.2
        d_out = W.shape[1]
        Wh = x @ W
        e_src = Wh @ a[:d_out]
        e_dst = Wh @ a[d_out:]
        e = jax.nn.leaky_relu(e_src[:, None] + e_dst[None, :], NEG_SLOPE)
        N = Wh.shape[0]
        mask = (adj > 0) | jnp.eye(N, dtype=bool)
        e = jnp.where(mask, e, NEG_INF)
        alpha = jax.nn.softmax(e, axis=1)
        h = alpha @ Wh
        return h

    def _L0_ffn_ref(x, Wr, br, ln_g, ln_b, W1, b1, W2, b2):
        import jax, jax.numpy as jnp
        import numpy as np
        TOP_K = 2
        LN_EPS = 1e-05
        B, S, D = x.shape
        N = B * S
        xt = x.reshape(N, D)
        logits = xt @ Wr + br
        probs = jax.nn.softmax(logits, axis=-1)
        top_p, top_idx = jax.lax.top_k(probs, TOP_K)
        weights = top_p / top_p.sum(axis=-1, keepdims=True)
        mu = xt.mean(axis=-1, keepdims=True)
        var = ((xt - mu) ** 2).mean(axis=-1, keepdims=True)
        xn = (xt - mu) * jax.lax.rsqrt(var + LN_EPS)
        xe = xn[None, :, :] * ln_g[:, None, :] + ln_b[:, None, :]
        h = jax.nn.gelu(jnp.einsum('end,edh->enh', xe, W1) + b1[:, None, :], approximate=False)
        y = jnp.einsum('enh,ehd->end', h, W2) + b2[:, None, :]
        y_tok = jnp.transpose(y, (1, 0, 2))
        sel = jnp.take_along_axis(y_tok, top_idx[:, :, None], axis=1)
        out = (weights[:, :, None] * sel).sum(axis=1)
        return out.reshape(B, S, D)

    x = x + _L0_gnn_ref(_layernorm(x, axis=-1), adj, L0_gnn_W, L0_gnn_a)
    x = x + _L0_ffn_ref((_layernorm(x, axis=-1))[None], L0_ffn_Wr, L0_ffn_br, L0_ffn_ln_g, L0_ffn_ln_b, L0_ffn_W1, L0_ffn_b1, L0_ffn_W2, L0_ffn_b2)[0]
    return x


_drawn_inputs = setup_inputs


def setup_inputs(seed=0):
    import zlib

    import numpy as np

    out = dict(_drawn_inputs(seed))
    spreads = {'L0_ffn_br': (0.0, 0.1),
     'L0_ffn_ln_g': (1.0, 0.2),
     'L0_ffn_ln_b': (0.0, 0.1),
     'L0_ffn_b1': (0.0, 0.1),
     'L0_ffn_b2': (0.0, 0.1)}
    factors = {}
    for name, (base, spread) in spreads.items():
        noise = np.random.default_rng([zlib.crc32(name.encode()), seed]).standard_normal(out[name].shape)
        drawn = base * np.exp(spread * noise) if base else spread * noise
        out[name] = jnp.asarray(drawn.astype(out[name].dtype))
    for name, factor in factors.items():
        out[name] = (out[name] * factor).astype(out[name].dtype)
    return out
```

```python
from contextlib import ExitStack

import concourse.bass as bass
from concourse import mybir

ALU = mybir.AluOpType
ACT = mybir.ActivationFunctionType
F32 = mybir.dt.float32
F16 = mybir.dt.float16
BF16 = mybir.dt.bfloat16
U32 = mybir.dt.uint32
I32 = mybir.dt.int32

P = 128
MASKED = -1.0e30
SLOPE = 0.2
LN_EPS = 1e-5
WSCALE = 256.0


def build(nc, x, adj, gnn_w, gnn_a, w_r, b_r, ln_g, ln_b, w1, b1, w2, b2, out):
    N, D = x.shape
    E = w_r.shape[1]
    HID = w1.shape[2]
    T = N // P
    KD = D // P
    HC = HID // P
    G = 4
    GJ = T // G
    GW = GJ * P
    HALF = N // 2
    REGION = N + P
    ROW = D + 1
    CHUNKS = 4
    CW = KD * HID // 2
    FT = 2 * N // P + E - 1
    assert D == 256 and HID == 1024 and E == 8 and CW == 1024 and T % 4 == 0 and FT % 2 == 1

    rows_dram = nc.dram_tensor("rows_dram", [E * REGION, ROW], F32, kind="Internal").ap()
    wsplit_dram = nc.dram_tensor("wsplit_dram", [E * CHUNKS, P, 2 * CW], F16, kind="Internal").ap()
    y_dram = nc.dram_tensor("y_dram", [2 * N + FT * P, D], F32, kind="Internal").ap()

    adj_tiles = adj.rearrange("(t p) n -> t p n", p=P)
    x_view = x.rearrange("(t p) d -> p t d", p=P)
    out_view = out.rearrange("(t p) d -> p t d", p=P)
    w1_view = w1.rearrange("e (k p) h -> e k p h", p=P)
    w2_view = w2.rearrange("e (q c p) d -> e q p c d", q=2, p=P)
    y_view = y_dram[0:2 * N, :].rearrange("(t p k) d -> p t (k d)", p=P, k=2)

    with ExitStack() as ctx:
        def sb(name, shape, dt, stack=ctx):
            return stack.enter_context(nc.sbuf_tensor(name, shape, dt))

        def sem(name):
            return ctx.enter_context(nc.semaphore(name))

        tp = [ctx.enter_context(nc.psum_tensor(f"tp{u}", [P, GW], F32)) for u in range(2)]
        acc = [ctx.enter_context(nc.psum_tensor(f"acc{u}", [P, 2 * D], F32)) for u in range(2)]
        xt_ps = ctx.enter_context(nc.psum_tensor("xt_ps", [P, 512], F32))
        rt_ps = ctx.enter_context(nc.psum_tensor("rt_ps", [P, 512], F32))

        x_all = sb("x_all", [P, T, D], F32)
        ident = sb("ident", [P, P], F32)
        top_all = sb("top_all", [P, T, 2], F32)
        gate = sb("gate", [P, 2, T], F32)
        count = sb("count", [P, E], F32)
        table_e = sb("table_e", [1, FT], I32)
        table_row = sb("table_row", [1, FT], I32)
        tail_row = sb("tail_row", [1, E], I32)
        g_cols = sb("g_cols", [P, E, KD], F32)
        b_cols = sb("b_cols", [P, E, KD], F32)
        b1_cols = sb("b1_cols", [P, E, HC], F32)
        small = sb("small", [P, 64], F32)
        iota_t = sb("iota_t", [P, FT], F32)
        tt_a = sb("tt_a", [P, FT], F32)
        tt_b = sb("tt_b", [P, FT], F32)
        tt_c = sb("tt_c", [P, FT], F32)
        zrow = sb("zrow", [P, ROW], F32)

        front = ExitStack()
        wh = sb("wh", [P, T, 2, D], F16, front)
        t_row = sb("t_row", [P, N], F32, front)
        adj_sb = [sb(f"adj_sb{u}", [P, N], F32, front) for u in range(2)]
        bias_sb = sb("bias_sb", [P, N], BF16, front)
        sc = [sb(f"sc{u}", [P, N], F32, front) for u in range(2)]
        pt_hi = [sb(f"pt_hi{g}", [P, GW], F16, front) for g in range(G)]
        pt_lo = [sb(f"pt_lo{g}", [P, GW], F16, front) for g in range(G)]
        wf = [sb(f"wf{u}", [P, CW], F32, front) for u in range(2)]
        wsp = [sb(f"wsp{u}", [P, 2 * CW], F16, front) for u in range(2)]
        xn = [sb(f"xn{u}", [P, D], F32, front) for u in range(2)]
        xnt = [sb(f"xnt{u}", [P, D], F32, front) for u in range(2)]
        wcat = sb("wcat", [P, KD, D + 2], F32, front)
        a_rep = sb("a_rep", [P, 2, D], F32, front)
        wa_rep = sb("wa_rep", [P, KD, P], F32, front)
        w_r_sb = sb("w_r_sb", [P, KD, E], F32, front)
        b_r_rep = sb("b_r_rep", [P, E], F32, front)
        stats = sb("stats", [P, T, 2], F32, front)
        bst = sb("bst", [P, 8], F32, front)
        rstd = sb("rstd", [P, T], F32, front)
        half_neg = sb("half_neg", [P, T], F32, front)
        s_col = sb("s_col", [P, T], F32, front)
        s_col2 = sb("s_col2", [P, T], F32, front)
        mx = sb("mx", [P, 2], F32, front)
        neg_m = [sb(f"neg_m{u}", [P, 1], F32, front) for u in range(2)]
        rsum = [sb(f"rsum{u}", [P, 1], F32, front) for u in range(2)]
        rinv = sb("rinv", [P, 1], F32, front)
        mv1 = sb("mv1", [P, 2], F32, front)
        mv2 = sb("mv2", [P, 2], F32, front)
        rs1 = sb("rs1", [P, 2], F32, front)
        rs2 = sb("rs2", [P, 2], F32, front)
        bs1 = sb("bs1", [P, 6], F32, front)
        bs2 = sb("bs2", [P, 6], F32, front)
        row_a = [sb(f"row_a{u}", [P, ROW], F32, front) for u in range(2)]
        row_b = [sb(f"row_b{u}", [P, ROW], F32, front) for u in range(2)]
        dest = sb("dest", [P, T, 2], F32, front)
        tri = sb("tri", [P, P], BF16, front)
        ones = sb("ones", [P, P], BF16, front)
        iota_e = sb("iota_e", [P, E], F32, front)
        lg = sb("lg", [P, E], F32, front)
        top8 = sb("top8", [P, 8], F32, front)
        idx8 = sb("idx8", [P, 8], U32, front)
        idxf = sb("idxf", [P, 2], F32, front)
        oh1 = sb("oh1", [P, E], F32, front)
        oh2 = sb("oh2", [P, E], F32, front)
        oh = sb("oh", [P, E], BF16, front)
        posb = sb("posb", [P, E], F32, front)
        junk = sb("junk", [P, E], F32, front)
        junk2 = sb("junk2", [P, E], F32, front)
        slotf = sb("slotf", [P, 2], F32, front)
        slot = [sb(f"slot{u}", [P, 2], U32, front) for u in range(2)]
        front.close()

        w_sb = sb("w_sb", [P, E * CHUNKS * 2 * CW], F16)
        b2_rep = sb("b2_rep", [P, E * D], F32)
        xs = [sb(f"xs{u}", [P, ROW], F32) for u in range(2)]
        xg = sb("xg", [P, D], F32)
        x_hi = [sb(f"x_hi{u}", [P, D], F16) for u in range(2)]
        x_lo = [sb(f"x_lo{u}", [P, D], F16) for u in range(2)]
        hf = [sb(f"hf{u}", [P, HID], F32) for u in range(2)]
        h_hi = [sb(f"h_hi{u}", [P, HID], F16) for u in range(2)]
        h_lo = [sb(f"h_lo{u}", [P, HID], F16) for u in range(2)]
        y_sb = [sb(f"y_sb{u}", [P, D], F32) for u in range(2)]
        dump = sb("dump", [P, 1], F32)
        dz = sb("dz", [P, 1], F32)
        yidx = [sb(f"yidx{u}", [P, 1], U32) for u in range(2)]
        yb = [sb(f"yb{u}", [P, 2, 2 * D], F32) for u in range(2)]

        s_x = [sem(f"x_loaded{c}") for c in range(4)]
        s_par = sem("params_loaded")
        s_pc = sem("pool_consts")
        s_ps = sem("pool_step")
        s_ds = sem("dve_step")
        s_fr = sem("dve_front_step")
        s_xc = sem("ffn_x_hi_done")
        s_hc = sem("ffn_h_hi_done")
        s_yc = sem("ffn_y_half")
        s_apart = sem("carries_a_register_wait")
        s_cb = sem("first_choice_added")
        s_st = sem("stats_done")
        s_rstd = sem("rstd_done")
        s_xn = sem("xn_done")
        s_xnt_ps = sem("xnt_in_psum")
        s_xnt = sem("xnt_in_sbuf")
        s_wa = sem("wa_done")
        s_wh = sem("wh_in_psum")
        s_whh = sem("wh_hi_done")
        s_whl = sem("wh_lo_done")
        s_tr = sem("t_row_part_done")
        s_s2 = sem("s_cols_done")
        s_adj = [sem(f"adj_loaded{u}") for u in range(2)]
        s_mask = sem("mask_done")
        s_q = sem("slope_branch_done")
        s_m = sem("neg_max_done")
        s_e = sem("exp_done")
        s_t = sem("p_transposed")
        s_hi = sem("p_hi_done")
        s_lo = sem("p_lo_done")
        s_av = sem("av_done")
        s_x1 = sem("x1_done")
        s_mv1 = sem("ln1_stats")
        s_r1 = sem("ln1_rstd")
        s_xl = sem("xl_done")
        s_xlp = sem("xl_t_in_psum")
        s_xlt = sem("xl_t_in_sbuf")
        s_mv2 = sem("ln2_stats")
        s_r2 = sem("ln2_rstd")
        s_row = sem("row_done")
        s_lg = sem("logits_done")
        s_oh = sem("onehot_done")
        s_pos = sem("positions_done")
        s_slot = sem("slots_done")
        s_sc = [sem(f"rows_scattered{u}") for u in range(2)]
        s_wf = [sem(f"w_chunk_loaded{u}") for u in range(2)]
        s_wsp = sem("w_chunk_split")
        s_wst = [sem(f"w_chunk_stored{u}") for u in range(2)]
        s_tab = sem("table_done")
        s_tail = sem("tails_zeroed")
        s_d = sem("gate_gap_done")
        s_ge = sem("gate_exp_done")
        s_wl = [sem(f"w_loaded{e}") for e in range(E)]
        s_wr = sem("w_ready_in_order")
        s_b2 = sem("b2_loaded")
        s_xs = [sem(f"xs_loaded{u}") for u in range(2)]
        s_xtp = sem("ffn_xt_in_psum")
        s_xg = sem("ffn_xt_scaled")
        s_xh = sem("ffn_x_split")
        s_g1 = sem("ffn_hidden_in_psum")
        s_ge1 = sem("ffn_gelu_done")
        s_hh = sem("ffn_hidden_split")
        s_g2 = sem("ffn_y_in_psum")
        s_y = sem("ffn_y_done")
        s_yi = sem("ffn_index_done")
        s_ysc = [sem(f"y_scattered{u}") for u in range(2)]
        s_yb = [sem(f"y_back{u}") for u in range(2)]
        s_fin = sem("final_done")
        s_out = sem("out_stored")

        block = ctx.enter_context(nc.Block())

        def chain(eng, sem_, base):
            n = [0]

            def link(ins):
                n[0] += 1
                ins.then_inc(sem_, 1)
                eng.wait_ge(sem_, base + n[0])
            return link, n

        def apart(eng):
            eng.sem_inc(s_apart, 1)

        TO = T // 2
        FO = (FT - 1) // 2

        @block.sync
        def _(sp):
            TC = T // 4
            for c in range(4):
                sp.dma_start(x_all[:, c * TC:(c + 1) * TC, :], x_view[:, c * TC:(c + 1) * TC, :]).then_inc(s_x[c], 16)
            params = [
                (wcat[:, :, 0:D], gnn_w.rearrange("(k p) n -> p k n", p=P)),
                (a_rep[:, :, :], gnn_a.rearrange("(o k d) -> o k d", o=1, k=2).broadcast_to([P, 2, D])),
                (w_r_sb[:, :, :], w_r.rearrange("(k p) e -> p k e", p=P)),
                (b_r_rep[:, :], b_r.rearrange("(o e) -> o e", o=1).broadcast_to([P, E])),
            ]
            for dst, src in params:
                sp.dma_start(dst, src).then_inc(s_par, 16)
            with nc.allow_non_contiguous_dma(reason="one column for each partition"):
                sp.dma_start(g_cols[:, :, :], ln_g.rearrange("e (k p) -> p e k", p=P)).then_inc(s_par, 16)
                sp.dma_start(b_cols[:, :, :], ln_b.rearrange("e (k p) -> p e k", p=P)).then_inc(s_par, 16)
                sp.dma_start(b1_cols[:, :, :], b1.rearrange("e (c p) -> p e c", p=P)).then_inc(s_par, 16)

            def load_adj(o, u):
                sp.dma_start(adj_sb[u][:, :], adj_tiles[2 * o + u]).then_inc(s_adj[u], 16)

            def load_w(e, q):
                src = w1_view[e, q] if q < 2 else w2_view[e, q - 2]
                dst = wf[q % 2][:, :]
                if q >= 2:
                    dst = dst.rearrange("p (c d) -> p c d", d=D)
                sp.dma_start(dst, src).then_inc(s_wf[q % 2], 16)

            def store_w(e, q):
                sp.wait_ge(s_wsp, CHUNKS * e + q + 1)
                sp.dma_start(wsplit_dram[CHUNKS * e + q], wsp[q % 2][:, :]).then_inc(s_wst[q % 2], 16)

            load_adj(0, 0)
            load_adj(0, 1)

            def steps(e, first=False, last=False):
                for q in range(CHUNKS):
                    i = CHUNKS * e + q
                    if not (last and q >= 2):
                        sp.wait_ge(s_mask, i + 1)
                        load_adj(2 * e + q // 2 + 1, q % 2)
                    if not (first and q < 2):
                        sp.wait_ge(s_wsp, i - 1)
                    load_w(e, q)
                    if q >= 1:
                        store_w(e, q - 1)
                    elif not first:
                        store_w(e - 1, CHUNKS - 1)

            steps(0, first=True)
            with sp.Fori(1, E - 1) as e:
                steps(e)
            steps(E - 1, last=True)
            store_w(E - 1, CHUNKS - 1)

            sp.wait_ge(s_av, G * T)
            sp.wait_ge(s_slot, T)
            for u in range(2):
                sp.wait_ge(s_wst[u], 16 * E * CHUNKS // 2)
                sp.wait_ge(s_sc[u], 32 * TO)
            for e in range(E):
                sp.dma_start(w_sb[:, e * CHUNKS * 2 * CW:(e + 1) * CHUNKS * 2 * CW].rearrange("p (q n) -> p q n", q=CHUNKS),
                             wsplit_dram[e * CHUNKS:(e + 1) * CHUNKS].rearrange("q p n -> p q n")).then_inc(s_wl[e], 16)
                if e == 0:
                    sp.dma_start(b2_rep[:, :], b2.rearrange("(o e) d -> o (e d)", o=1).broadcast_to([P, E * D])).then_inc(s_b2, 16)
                    sp.wait_ge(s_tab, 1)
                    for k in range(E):
                        row = sp.value_load(tail_row[0:1, k:k + 1], min_val=0, max_val=E * REGION - P)
                        sp.dma_start(rows_dram[bass.ds(row, P), :], zrow[:, :]).then_inc(s_tail, 16)
            for e in range(E):
                sp.wait_ge(s_wl[e], 16)
                sp.sem_inc(s_wr, 1)

            sp.wait_ge(s_ysc[0], 16 * (FO + 1))
            sp.wait_ge(s_ysc[1], 16 * FO)

            def load_y(o, u, ringed=True):
                if ringed:
                    sp.wait_ge(s_fin, 2 * o + u - 1)
                sp.dma_start(yb[u][:, :, :], y_view[:, bass.ds((2 * o + u) * 2, 2), :]).then_inc(s_yb[u], 16)

            def store_out(o, u):
                sp.wait_ge(s_fin, 2 * o + u + 1)
                sp.dma_start(out_view[:, bass.ds((2 * o + u) * 2, 2), :], x_all[:, bass.ds((2 * o + u) * 2, 2), :]).then_inc(s_out, 16)

            load_y(0, 0, False)
            load_y(0, 1, False)
            with sp.Fori(1, T // 4) as o:
                load_y(o, 0)
                store_out(o - 1, 0)
                load_y(o, 1)
                store_out(o - 1, 1)
            store_out(T // 4 - 1, 0)
            store_out(T // 4 - 1, 1)
            sp.wait_ge(s_out, 16 * T // 2)
            for u in range(2):
                sp.wait_ge(s_adj[u], 16 * TO)

        @block.gpsimd
        def _(pool):
            pool.memset(ident[:, :], 0.0).then_inc(s_ps, 1)
            pool.memset(tri[:, :], 1.0).then_inc(s_ps, 1)
            pool.memset(half_neg[:, :], -0.5).then_inc(s_ps, 1)
            pool.memset(ones[:, :], 1.0).then_inc(s_ps, 1)
            pool.memset(zrow[:, :], 0.0).then_inc(s_ps, 1)
            pool.wait_ge(s_ps, 5)
            pool.affine_select(out=ident[:, :], in_=ident[:, :], compare_op=ALU.not_equal, fill=1.0, base=0,
                               pattern=[[-1, P]], channel_multiplier=1).then_inc(s_pc, 1)
            pool.affine_select(out=tri[:, :], in_=tri[:, :], compare_op=ALU.is_gt, fill=0.0, base=0,
                               pattern=[[1, P]], channel_multiplier=-1).then_inc(s_pc, 1)
            pool.iota(iota_e[:, :], [[1, E]], base=0, channel_multiplier=0,
                      allow_small_or_imprecise_dtypes=True).then_inc(s_pc, 1)
            pool.iota(count[:, :], [[REGION, E]], base=0, channel_multiplier=0,
                      allow_small_or_imprecise_dtypes=True).then_inc(s_pc, 1)
            pool.iota(iota_t[:, :], [[1, FT]], base=0, channel_multiplier=0,
                      allow_small_or_imprecise_dtypes=True).then_inc(s_pc, 1)
            pool.iota(dest[:, :, :], [[2 * P, T], [1, 2]], base=1, channel_multiplier=2,
                      allow_small_or_imprecise_dtypes=True).then_inc(s_pc, 1)
            pool.wait_ge(s_st, T + 1)
            pool.wait_ge(s_pc, 6)
            pool.tensor_scalar(rstd[:, :], stats[:, :, 1], 1.0, LN_EPS, ALU.mult, ALU.add).then_inc(s_ps, 1)
            pool.wait_ge(s_ps, 6)
            pool.tensor_tensor(rstd[:, :], rstd[:, :], half_neg[:, :], ALU.pow).then_inc(s_rstd, 1)
            STEP0 = 6
            STEPS = 7

            def step(e, q, first):
                i = CHUNKS * e + q
                u = q % 2
                base = i * STEPS + STEP0
                pool.wait_ge(s_mv1, i + 1)
                apart(pool)
                pool.tensor_scalar(rs1[:, 0:1], mv1[:, 1:2], 1.0, LN_EPS, ALU.mult, ALU.add).then_inc(s_ps, 1)
                pool.wait_ge(s_ps, base + 1)
                pool.tensor_tensor(rs1[:, 1:2], rs1[:, 0:1], half_neg[:, 0:1], ALU.pow).then_inc(s_r1, 1)
                pool.wait_ge(s_mv2, i + 1)
                apart(pool)
                pool.tensor_scalar(rs2[:, 0:1], mv2[:, 1:2], 1.0, LN_EPS, ALU.mult, ALU.add).then_inc(s_ps, 1)
                pool.wait_ge(s_ps, base + 2)
                pool.tensor_tensor(rs2[:, 1:2], rs2[:, 0:1], half_neg[:, 0:1], ALU.pow).then_inc(s_r2, 1)
                pool.wait_ge(s_row, i + 1)
                apart(pool)
                pool.tensor_copy(row_b[u][:, 0:D], row_a[u][:, 0:D]).then_inc(s_ps, 1)
                apart(pool)
                pool.tensor_copy(row_a[u][:, D:ROW], dest[:, bass.ds(i, 1), 0]).then_inc(s_ps, 1)
                apart(pool)
                pool.tensor_copy(row_b[u][:, D:ROW], dest[:, bass.ds(i, 1), 1]).then_inc(s_ps, 1)
                pool.wait_ge(s_ps, base + 5)
                pool.wait_ge(s_slot, i + 1)
                for k, rows in enumerate((row_a, row_b)):
                    apart(pool)
                    pool.indirect_dma_start(
                        out=rows_dram[:, :], out_offset=bass.IndirectOffsetOnAxis(ap=slot[u][:, k:k + 1], axis=0),
                        in_=rows[u][:, :], in_offset=None).then_inc(s_sc[u], 16)
                pool.wait_ge(s_wf[u], 16 * (2 * e + q // 2 + 1))
                if not (first and q < 2):
                    pool.wait_ge(s_wst[u], 16 * (2 * e + q // 2))
                apart(pool)
                pool.tensor_scalar(wf[u][:, :], wf[u][:, :], WSCALE, 0.0, ALU.mult, ALU.add).then_inc(s_ps, 1)
                pool.wait_ge(s_ps, base + 6)
                apart(pool)
                pool.tensor_copy(wsp[u][:, 0:CW], wf[u][:, :]).then_inc(s_ps, 1)
                pool.wait_ge(s_ps, base + 7)
                pool.tensor_tensor(wsp[u][:, CW:2 * CW], wf[u][:, :], wsp[u][:, 0:CW], ALU.subtract).then_inc(s_wsp, 1)

            for q in range(CHUNKS):
                step(0, q, True)
            with pool.Fori(1, E) as e:
                for q in range(CHUNKS):
                    step(e, q, False)

            base = STEP0 + T * STEPS
            for u in range(2):
                pool.wait_ge(s_sc[u], 32 * TO)
            pool.wait_ge(s_av, G * T)
            pool.iota(dump[:, :], [[0, 1]], base=2 * N + 1, channel_multiplier=1,
                      allow_small_or_imprecise_dtypes=True).then_inc(s_ps, 1)
            base += 1

            def index(o, u, t, ringed=True):
                b = 2 * t + base
                pool.wait_ge(s_xs[u], 16 * (o + 1))
                pool.wait_ge(s_ps, b)
                if ringed != "first":
                    pool.wait_ge(s_yi, t)
                apart(pool)
                pool.tensor_scalar(dz[:, :], xs[u][:, D:ROW], 0.0, dump[:, 0:1], ALU.is_equal, ALU.mult).then_inc(s_ps, 1)
                pool.wait_ge(s_ps, b + 1)
                apart(pool)
                pool.tensor_scalar(dump[:, :], dump[:, :], 1.0, float(P), ALU.mult, ALU.add).then_inc(s_ps, 1)
                if ringed is True:
                    pool.wait_ge(s_ysc[u], 16 * o)
                apart(pool)
                pool.tensor_scalar(yidx[u][:, :], xs[u][:, D:ROW], -1.0, dz[:, 0:1], ALU.add, ALU.add).then_inc(s_yi, 1)

            def scatter(u, t):
                pool.wait_ge(s_yi, t + 1)
                pool.wait_ge(s_y, t + 1)
                apart(pool)
                pool.indirect_dma_start(
                    out=y_dram[:, :], out_offset=bass.IndirectOffsetOnAxis(ap=yidx[u][:, 0:1], axis=0),
                    in_=y_sb[u][:, :], in_offset=None).then_inc(s_ysc[u], 16)

            index(0, 0, 0, "first")
            index(0, 1, 1, False)
            scatter(0, 0)
            with pool.Fori(1, FO) as o:
                index(o, 0, 2 * o)
                scatter(1, 2 * o - 1)
                index(o, 1, 2 * o + 1)
                scatter(0, 2 * o)
            index(FO, 0, FT - 1)
            scatter(1, FT - 2)
            scatter(0, FT - 1)

        @block.tensor
        def _(pe):
            pe.wait_ge(s_pc, 2)

            def project(o, u, prev, ringed):
                i = 2 * o + u
                if i is not None and prev != "tail":
                    pe.wait_ge(s_xn, i + 1)
                    if ringed:
                        pe.wait_ge(s_xnt, i - 1)
                    for k in range(KD):
                        m = pe.transpose(tp[u][:, k * P:(k + 1) * P], xn[u][:, k * P:(k + 1) * P], ident[:, :])
                    m.then_inc(s_xnt_ps, 1)
                if prev is None:
                    return
                v = 1 - u
                pe.wait_ge(s_xnt, i)
                if ringed == 2:
                    pe.wait_ge(s_whl, i - 2)
                    pe.wait_ge(s_tr, i - 2)
                for k in range(KD):
                    pe.matmul(tp[v][:, 512:512 + D + 2], xnt[v][:, k * P:(k + 1) * P], wcat[:, k, :],
                              start=(k == 0), stop=(k == KD - 1))
                for k in range(KD):
                    m = pe.matmul(acc[v][:, 0:P], wa_rep[:, k, :], xnt[v][:, k * P:(k + 1) * P],
                                  start=(k == 0), stop=(k == KD - 1))
                m.then_inc(s_wh, 1)

            project(0, 0, None, 0)
            pe.wait_ge(s_wa, 1)
            project(0, 1, True, 0)
            project(1, 0, True, 1)
            project(1, 1, True, 2)
            with pe.Fori(2, TO) as o:
                project(o, 0, True, 2)
                project(o, 1, True, 2)
            project(TO, 0, "tail", 2)

            def p_transpose(o, u, g, ringed=True):
                i = 2 * o + u
                if g == 0:
                    pe.wait_ge(s_e, i + 1)
                if ringed:
                    pe.wait_ge(s_lo, G * i + g - 1)
                for c in range(GJ):
                    m = pe.transpose(tp[g % 2][:, c * P:(c + 1) * P], sc[u][:, (GJ * g + c) * P:(GJ * g + c + 1) * P], ident[:, :])
                m.then_inc(s_t, 1)

            def av(o, u, g, ringed=True):
                i = 2 * o + u
                pe.wait_ge(s_lo, G * i + g + 1)
                if g == 0 and ringed:
                    pe.wait_ge(s_x1, i - 1)
                for c in range(GJ):
                    j = GJ * g + c
                    first = g == 0 and c == 0
                    last = g == G - 1 and c == GJ - 1
                    pe.matmul(acc[u][:, :], pt_hi[g][:, c * P:(c + 1) * P], wh[:, j, :, :],
                              start=first, stop=False, skip_group_check=True)
                    m = pe.matmul(acc[u][:, 0:D], pt_lo[g][:, c * P:(c + 1) * P], wh[:, j, 0, :],
                                  start=False, stop=last, skip_group_check=True)
                m.then_inc(s_av, 1)

            def router_t(i):
                pe.wait_ge(s_xl, i + 1)
                for k in range(KD):
                    m = pe.transpose(xt_ps[:, k * P:(k + 1) * P], xn[0][:, k * P:(k + 1) * P], ident[:, :])
                m.then_inc(s_xlp, 1)

            def router_mm(i):
                pe.wait_ge(s_xlt, i + 1)
                for k in range(KD):
                    m = pe.matmul(rt_ps[:, 0:E], xnt[0][:, k * P:(k + 1) * P], w_r_sb[:, k, :], start=(k == 0), stop=(k == KD - 1))
                m.then_inc(s_lg, 1)

            def router_pos(i):
                pe.wait_ge(s_oh, i + 1)
                pe.matmul(rt_ps[:, 16:16 + E], tri[:, :], oh[:, :], start=True, stop=True)
                pe.matmul(rt_ps[:, 32:32 + E], ones[:, :], oh[:, :], start=True, stop=True).then_inc(s_pos, 1)

            def attend(o, u, first=False, second=False):
                i = 2 * o + u
                p_transpose(o, u, 0, not first)
                if not first:
                    av(o - 1 + u, 1 - u, 3)
                p_transpose(o, u, 1, not first)
                av(o, u, 0, not (first or second))
                if not first:
                    router_t(i - 1)
                p_transpose(o, u, 2)
                av(o, u, 1)
                if not first:
                    router_mm(i - 1)
                p_transpose(o, u, 3)
                av(o, u, 2)
                if not first:
                    router_pos(i - 1)

            pe.wait_ge(s_whl, T)
            attend(0, 0, first=True)
            attend(0, 1, second=True)
            with pe.Fori(1, TO) as o:
                attend(o, 0)
                attend(o, 1)
            av(TO - 1, 1, 3)
            router_t(T - 1)
            router_mm(T - 1)
            router_pos(T - 1)

            def ffn_t(o, u, t, ringed=True):
                pe.wait_ge(s_xs[u], 16 * (o + 1))
                if ringed:
                    pe.wait_ge(s_xg, t)
                for k in range(KD):
                    m = pe.transpose(xt_ps[:, k * P:(k + 1) * P], xs[u][:, k * P:(k + 1) * P], ident[:, :])
                m.then_inc(s_xtp, 1)

            def expert_of(t):
                return pe.value_load(table_e[0:1, bass.ds(t, 1)], min_val=0, max_val=E - 1)

            def up(u, t, e, ringed=True):
                pe.wait_ge(s_wr, e + 1)
                pe.wait_ge(s_xh, t + 1)
                if ringed:
                    pe.wait_ge(s_ge1, t - 1)
                for c in range(HC):
                    for k in range(KD):
                        at = e * (CHUNKS * 2 * CW) + k * 2 * CW + c * P
                        w_hi = w_sb[:, bass.ds(at, P)]
                        w_lo = w_sb[:, bass.ds(at + CW, P)]
                        o = tp[u][:, c * P:(c + 1) * P]
                        bank = c % 4 == 0 and k == 0
                        pe.matmul(o, w_hi, x_hi[u][:, k * P:(k + 1) * P], start=bank, stop=False, skip_group_check=True)
                        pe.matmul(o, w_hi, x_lo[u][:, k * P:(k + 1) * P], start=False, stop=False, skip_group_check=True)
                        m = pe.matmul(o, w_lo, x_hi[u][:, k * P:(k + 1) * P], start=False, stop=(k == KD - 1), skip_group_check=True)
                m.then_inc(s_g1, 1)

            def down(u, t, e, ringed=True):
                pe.wait_ge(s_hh, t + 1)
                if ringed:
                    pe.wait_ge(s_y, t - 1)
                for c in range(HC):
                    at = e * (CHUNKS * 2 * CW) + (2 + c // 4) * 2 * CW + (c % 4) * D
                    w_hi = w_sb[:, bass.ds(at, D)]
                    w_lo = w_sb[:, bass.ds(at + CW, D)]
                    pe.matmul(acc[u][:, 0:D], h_hi[u][:, c * P:(c + 1) * P], w_hi, start=(c == 0), stop=False, skip_group_check=True)
                    pe.matmul(acc[u][:, D:2 * D], h_hi[u][:, c * P:(c + 1) * P], w_lo, start=False, stop=False, skip_group_check=True)
                    m = pe.matmul(acc[u][:, 0:D], h_lo[u][:, c * P:(c + 1) * P], w_hi, start=False, stop=(c == HC - 1), skip_group_check=True)
                m.then_inc(s_g2, 1)

            pe.wait_ge(s_tab, 1)
            ffn_t(0, 0, 0, False)
            up(0, 0, expert_of(0), False)
            ffn_t(0, 1, 1)
            up(1, 1, expert_of(1), False)
            ffn_t(1, 0, 2)
            down(0, 0, expert_of(0), False)
            up(0, 2, expert_of(2))
            ffn_t(1, 1, 3)
            down(1, 1, expert_of(1), False)
            with pe.Fori(1, FO - 1) as o:
                up(1, 2 * o + 1, expert_of(2 * o + 1))
                ffn_t(o + 1, 0, 2 * o + 2)
                down(0, 2 * o, expert_of(2 * o))
                up(0, 2 * o + 2, expert_of(2 * o + 2))
                ffn_t(o + 1, 1, 2 * o + 3)
                down(1, 2 * o + 1, expert_of(2 * o + 1))
            up(1, FT - 2, expert_of(FT - 2))
            ffn_t(FO, 0, FT - 1)
            down(0, FT - 3, expert_of(FT - 3))
            up(0, FT - 1, expert_of(FT - 1))
            down(1, FT - 2, expert_of(FT - 2))
            down(0, FT - 1, expert_of(FT - 1))

        @block.scalar
        def _(act):
            def project(o, u, part, ringed=True):
                i = 2 * o + u
                if part != "tail":
                    act.wait_ge(s_xnt_ps, i + 1)
                    if ringed:
                        act.wait_ge(s_wh, i - 1)
                    act.activation(xnt[u][:, :], tp[u][:, 0:D], ACT.Copy).then_inc(s_xnt, 1)
                if part != "head":
                    v = 1 - u
                    act.wait_ge(s_wh, i)
                    act.activation(wh[:, bass.ds(i - 1, 1), 0, :], tp[v][:, 512:512 + D], ACT.Copy).then_inc(s_whh, 1)
                    act.activation(t_row[:, bass.ds((i - 1) * P, P)], acc[v][:, 0:P], ACT.Copy).then_inc(s_tr, 1)

            project(0, 0, "head", False)
            project(0, 1, "", False)
            with act.Fori(1, TO) as o:
                project(o, 0, "")
                project(o, 1, "")
            project(TO, 0, "tail")

            def branch(o, u, half, ringed=True):
                i = 2 * o + u
                if half == 0 and ringed:
                    act.wait_ge(s_t, G * (i - 1))
                cols = slice(half * HALF, (half + 1) * HALF)
                act.activation(sc[u][:, cols], t_row[:, cols], ACT.Identity, bias=s_col2[:, bass.ds(i, 1)],
                               scale=SLOPE).then_inc(s_q, 1)

            def exps(o, u):
                i = 2 * o + u
                act.wait_ge(s_m, i + 1)
                act.activation(sc[u][:, :], sc[u][:, :], ACT.Exp, bias=neg_m[u][:, 0:1], scale=1.0,
                               accum_out=rsum[u][:, 0:1]).then_inc(s_e, 1)

            def p_hi(o, u, g, ringed=True):
                i = 2 * o + u
                act.wait_ge(s_t, G * i + g + 1)
                if ringed:
                    act.wait_ge(s_av, G * i + g - 3)
                act.activation(pt_hi[g][:, :], tp[g % 2][:, :], ACT.Copy).then_inc(s_hi, 1)

            def router(i, ringed=True):
                act.wait_ge(s_xlp, i + 1)
                act.activation(xnt[0][:, :], xt_ps[:, 0:D], ACT.Copy).then_inc(s_xlt, 1)

            def attend(o, u, first=False, last=False, second=False):
                n, v = (o + u, 1 - u)
                p_hi(o, u, 0, not first)
                if not last:
                    branch(n, v, 0, not first)
                p_hi(o, u, 1, not first)
                if not last:
                    branch(n, v, 1)
                p_hi(o, u, 2, not first)
                if not first:
                    router(2 * o + u - 1)
                p_hi(o, u, 3, not first)
                if not last:
                    exps(n, v)

            act.wait_ge(s_s2, 1)
            act.wait_ge(s_tr, T)
            branch(0, 0, 0, False)
            branch(0, 0, 1, False)
            exps(0, 0)
            attend(0, 0, first=True)
            attend(0, 1)
            with act.Fori(1, TO - 1) as o:
                attend(o, 0)
                attend(o, 1)
            attend(TO - 1, 0)
            attend(TO - 1, 1, last=True)
            router(T - 1)
            act.wait_ge(s_d, 1)
            act.activation(gate[:, 1, :], gate[:, 0, :], ACT.Exp).then_inc(s_ge, 1)

            def load_x(o, u, t, ringed=True):
                if ringed:
                    act.wait_ge(s_xtp, t - 1)
                    act.wait_ge(s_yi, t - 1)
                row = act.value_load(table_row[0:1, bass.ds(t, 1)], min_val=0, max_val=E * REGION - P)
                act.dma_start(xs[u][:, :], rows_dram[bass.ds(row, P), :]).then_inc(s_xs[u], 16)

            def expert_of(t):
                return act.value_load(table_e[0:1, bass.ds(t, 1)], min_val=0, max_val=E - 1)

            def scaled(t, ringed=True):
                e = expert_of(t)
                act.wait_ge(s_xtp, t + 1)
                if ringed:
                    act.wait_ge(s_xh, t)
                for k in range(KD):
                    ins = act.activation(xg[:, k * P:(k + 1) * P], xt_ps[:, k * P:(k + 1) * P], ACT.Identity,
                                         bias=b_cols[:, bass.ds(e, 1), k], scale=g_cols[:, bass.ds(e, 1), k])
                ins.then_inc(s_xg, 1)

            def gelu(u, t, ringed=True):
                e = expert_of(t)
                act.wait_ge(s_g1, t + 1)
                if ringed:
                    act.wait_ge(s_hh, t - 1)
                for c in range(HC):
                    ins = act.activation(hf[u][:, c * P:(c + 1) * P], tp[u][:, c * P:(c + 1) * P], ACT.Gelu,
                                         bias=b1_cols[:, bass.ds(e, 1), c], scale=1.0 / WSCALE)
                ins.then_inc(s_ge1, 1)

            act.wait_ge(s_tab, 1)
            for u in range(2):
                act.wait_ge(s_sc[u], 32 * TO)
            act.wait_ge(s_tail, 16 * E)
            act.wait_ge(s_av, G * T)
            load_x(0, 0, 0, False)
            load_x(0, 1, 1, False)
            scaled(0, False)
            load_x(1, 0, 2)
            scaled(1)
            gelu(0, 0, False)
            load_x(1, 1, 3)
            scaled(2)
            gelu(1, 1, False)
            with act.Fori(1, FO - 1) as o:
                load_x(o + 1, 0, 2 * o + 2)
                scaled(2 * o + 1)
                gelu(0, 2 * o)
                load_x(o + 1, 1, 2 * o + 3)
                scaled(2 * o + 2)
                gelu(1, 2 * o + 1)
            load_x(FO, 0, FT - 1)
            scaled(FT - 2)
            gelu(0, FT - 3)
            scaled(FT - 1)
            gelu(1, FT - 2)
            gelu(0, FT - 1)

        @block.vector
        def _(dve):
            TC = T // 4
            dve.memset(bst[:, :], 0.0).then_inc(s_st, 1)
            for c in range(4):
                dve.wait_ge(s_x[c], 16)
                with dve.Fori(c * TC, (c + 1) * TC) as i:
                    dve.wait_ge(s_st, i + 1)
                    apart(dve)
                    dve.bn_stats(bst[:, 0:6], x_all[:, bass.ds(i, 1), :].rearrange("p a d -> p (a d)")).then_inc(s_ds, 1)
                    dve.wait_ge(s_ds, 2 * i + 1)
                    apart(dve)
                    dve.bn_aggr(bst[:, 6:8], bst[:, 0:6]).then_inc(s_ds, 1)
                    dve.wait_ge(s_ds, 2 * i + 2)
                    apart(dve)
                    dve.tensor_copy(stats[:, bass.ds(i, 1), :].rearrange("p a d -> p (a d)"), bst[:, 6:8]).then_inc(s_st, 1)
            dve.wait_ge(s_par, 16 * 7)
            dve.wait_ge(s_pc, 6)
            link, n = chain(dve, s_ds, 2 * T)
            for k in range(KD):
                for h in range(2):
                    link(dve.tensor_tensor_reduce(xnt[0][:, :], wcat[:, k, 0:D], a_rep[:, h, :], 1.0, 0.0,
                                                  ALU.mult, ALU.add, wcat[:, k, D + h:D + h + 1]))
            for k in range(KD):
                ins = dve.tensor_scalar(wa_rep[:, k, :], ones[:, :], wcat[:, k, D + 1:D + 2], None, ALU.mult)
                if k == KD - 1:
                    ins.then_inc(s_wa, 1)
            base = 2 * T + n[0]
            dve.wait_ge(s_wa, 1)
            dve.wait_ge(s_rstd, 1)

            def normed(o, u, ringed=True):
                i = 2 * o + u
                if ringed:
                    dve.wait_ge(s_xnt_ps, i - 1)
                dve.tensor_scalar(xn[u][:, :], x_all[:, bass.ds(i, 1), :].rearrange("p a d -> p (a d)"),
                                  stats[:, bass.ds(i, 1), 0], rstd[:, bass.ds(i, 1)], ALU.subtract, ALU.mult).then_inc(s_xn, 1)

            def split_wh(o, u):
                i = 2 * o + u
                dve.wait_ge(s_whh, i + 1)
                dve.tensor_copy(s_col[:, bass.ds(i, 1)], tp[u][:, 512 + D:512 + D + 1])
                dve.tensor_tensor(wh[:, bass.ds(i, 1), 1, :], tp[u][:, 512:512 + D], wh[:, bass.ds(i, 1), 0, :],
                                  ALU.subtract).then_inc(s_whl, 1)

            normed(0, 0, False)
            normed(0, 1, False)
            split_wh(0, 0)
            with dve.Fori(1, TO) as o:
                normed(o, 0)
                split_wh(o - 1, 1)
                normed(o, 1)
                split_wh(o, 0)
            split_wh(TO - 1, 1)
            dve.wait_ge(s_whl, T)
            dve.tensor_scalar(s_col2[:, :], s_col[:, :], SLOPE, None, ALU.mult).then_inc(s_s2, 1)
            dve.wait_ge(s_s2, 1)
            dve.wait_ge(s_tr, T)

            FRONT, POST = 3, 12

            def mask(o, u):
                i = 2 * o + u
                dve.wait_ge(s_adj[u], 16 * (o + 1))
                diag = adj_sb[u][:, bass.ds(i * P, P)]
                dve.tensor_tensor(diag, diag, ident[:, :], ALU.max).then_inc(s_fr, 1)
                dve.wait_ge(s_fr, i * FRONT + 1)
                dve.tensor_scalar(bias_sb[:, :], adj_sb[u][:, :], 0.0, MASKED, ALU.is_le, ALU.mult).then_inc(s_mask, 1)

            def leaky(o, u, half):
                i = 2 * o + u
                dve.wait_ge(s_q, 2 * i + half + 1)
                cols = slice(half * HALF, (half + 1) * HALF)
                ins = dve.scalar_tensor_tensor(out=sc[u][:, cols], in0=t_row[:, cols], scalar=s_col[:, bass.ds(i, 1)],
                                               in1=sc[u][:, cols], op0=ALU.add, op1=ALU.max)
                if half == 1:
                    ins.then_inc(s_fr, 1)

            def masked_max(o, u, half):
                i = 2 * o + u
                if half == 0:
                    dve.wait_ge(s_fr, i * FRONT + 2)
                    dve.wait_ge(s_mask, i + 1)
                cols = slice(half * HALF, (half + 1) * HALF)
                apart(dve)
                ins = dve.tensor_tensor_reduce(sc[u][:, cols], sc[u][:, cols], bias_sb[:, cols], 1.0, -3.0e38,
                                               ALU.add, ALU.max, mx[:, half:half + 1])
                if half == 1:
                    ins.then_inc(s_fr, 1)
                    dve.wait_ge(s_fr, i * FRONT + 3)
                    dve.tensor_scalar(neg_m[u][:, :], mx[:, 0:1], mx[:, 1:2], -1.0, ALU.max, ALU.mult).then_inc(s_m, 1)

            def p_lo(o, u, g):
                dve.wait_ge(s_hi, G * (2 * o + u) + g + 1)
                dve.tensor_tensor(pt_lo[g][:, :], tp[g % 2][:, :], pt_hi[g][:, :], ALU.subtract).then_inc(s_lo, 1)

            POST0 = base

            def post(o, u, stage, ringed=True):
                i = 2 * o + u
                start = {1: 0, 2: 4, 3: 5, 4: 5, 5: 10}[stage]
                done = {1: 4, 2: 5, 3: 5, 4: 10, 5: 12}[stage]
                link, n = chain(dve, s_ds, POST0 + i * POST + start)
                xi = x_all[:, bass.ds(i, 1), :].rearrange("p a d -> p (a d)")
                if stage == 1:
                    dve.wait_ge(s_av, G * i + G)
                    dve.wait_ge(s_e, i + 1)
                    link(dve.reciprocal(rinv[:, :], rsum[u][:, :]))
                    link(dve.scalar_tensor_tensor(out=xi, in0=acc[u][:, 0:D], scalar=rinv[:, 0:1], in1=xi, op0=ALU.mult, op1=ALU.add))
                    dve.scalar_tensor_tensor(out=xi, in0=acc[u][:, D:2 * D], scalar=rinv[:, 0:1], in1=xi, op0=ALU.mult,
                                             op1=ALU.add).then_inc(s_x1, 1)
                    dve.wait_ge(s_x1, i + 1)
                    apart(dve)
                    link(dve.bn_stats(bs1[:, :], xi))
                    if ringed:
                        dve.wait_ge(s_r1, i)
                    apart(dve)
                    dve.bn_aggr(mv1[:, :], bs1[:, :]).then_inc(s_mv1, 1)
                    dve.wait_ge(s_mv1, i + 1)
                    link(dve.tensor_copy(junk[:, 0:1], rinv[:, :]))
                if stage == 2:
                    dve.wait_ge(s_r1, i + 1)
                    if ringed:
                        dve.wait_ge(s_xlp, i)
                    dve.tensor_scalar(xn[0][:, :], xi, mv1[:, 0:1], rs1[:, 1:2], ALU.subtract, ALU.mult).then_inc(s_xl, 1)
                    dve.wait_ge(s_xl, i + 1)
                    apart(dve)
                    link(dve.bn_stats(bs2[:, :], xn[0][:, :]))
                    apart(dve)
                    dve.bn_aggr(mv2[:, :], bs2[:, :]).then_inc(s_mv2, 1)
                if stage == 3:
                    dve.wait_ge(s_r2, i + 1)
                    dve.wait_ge(s_mv2, i + 1)
                    if ringed == 2:
                        dve.wait_ge(s_sc[u], 32 * o)
                    dve.tensor_scalar(row_a[u][:, 0:D], xn[0][:, :], mv2[:, 0:1], rs2[:, 1:2], ALU.subtract,
                                      ALU.mult).then_inc(s_row, 1)
                if stage == 4:
                    dve.wait_ge(s_lg, i + 1)
                    link(dve.tensor_tensor(lg[:, :], rt_ps[:, 0:E], b_r_rep[:, :], ALU.add))
                    apart(dve)
                    link(dve.max(top8[:, :], lg[:, :]))
                    apart(dve)
                    link(dve.max_index(idx8[:, :], top8[:, :], lg[:, :]))
                    dve.tensor_copy(top_all[:, bass.ds(i, 1), :].rearrange("p a d -> p (a d)"), top8[:, 0:2])
                    link(dve.tensor_copy(idxf[:, :], idx8[:, 0:2]))
                    dve.tensor_scalar(oh1[:, :], iota_e[:, :], idxf[:, 0:1], None, ALU.is_equal)
                    link(dve.tensor_scalar(oh2[:, :], iota_e[:, :], idxf[:, 1:2], None, ALU.is_equal))
                    dve.tensor_tensor(oh[:, :], oh1[:, :], oh2[:, :], ALU.add).then_inc(s_oh, 1)
                if stage == 5:
                    dve.wait_ge(s_pos, i + 1)
                    link(dve.tensor_tensor(posb[:, :], rt_ps[:, 16:16 + E], count[:, :], ALU.add))
                    dve.tensor_tensor(count[:, :], rt_ps[:, 32:32 + E], count[:, :], ALU.add)
                    dve.tensor_tensor_reduce(junk2[:, :], oh1[:, :], posb[:, :], 1.0, 0.0, ALU.mult, ALU.add, slotf[:, 0:1])
                    link(dve.tensor_tensor_reduce(junk[:, :], oh2[:, :], posb[:, :], 1.0, 0.0, ALU.mult, ALU.add, slotf[:, 1:2]))
                    dve.tensor_copy(slot[u][:, :], slotf[:, :]).then_inc(s_slot, 1)
                assert start + n[0] == done, (stage, n[0])

            def attend(o, u, front=True, back=True, ring=2):
                n, v = (o + u, 1 - u)
                b, w = (o - 1 + u, 1 - u)
                if front:
                    mask(n, v)
                p_lo(o, u, 0)
                if back:
                    post(b, w, 1, ring > 0)
                if front:
                    leaky(n, v, 0)
                p_lo(o, u, 1)
                if back:
                    post(b, w, 2, ring > 0)
                if front:
                    leaky(n, v, 1)
                p_lo(o, u, 2)
                if back:
                    post(b, w, 3, ring)
                if front:
                    masked_max(n, v, 0)
                if back:
                    post(b, w, 4, ring > 0)
                p_lo(o, u, 3)
                if front:
                    masked_max(n, v, 1)
                if back:
                    post(b, w, 5, ring > 0)

            mask(0, 0)
            for half in range(2):
                leaky(0, 0, half)
            for half in range(2):
                masked_max(0, 0, half)
            attend(0, 0, back=False)
            attend(0, 1, ring=0)
            attend(1, 0, ring=1)
            attend(1, 1)
            with dve.Fori(2, TO - 1) as o:
                attend(o, 0)
                attend(o, 1)
            attend(TO - 1, 0)
            attend(TO - 1, 1, front=False)
            for stage in range(1, 6):
                post(TO - 1, 1, stage, 2)

            link, n = chain(dve, s_ds, POST0 + T * POST)
            cnt, til, cum, last = small[:, 0:E], small[:, E:2 * E], small[:, 2 * E:3 * E], small[:, 3 * E:3 * E + 1]
            tmp, one = small[:, 32:32 + E], small[:, 40:40 + E]
            link(dve.tensor_copy(tail_row[0:1, :], count[0:1, :]))
            link(dve.scalar_tensor_tensor(out=cnt, in0=iota_e[:, :], scalar=-float(REGION), in1=count[:, :], op0=ALU.mult, op1=ALU.add))
            link(dve.tensor_scalar(tmp.bitcast(I32), cnt, 63.5, 1.0 / P, ALU.add, ALU.mult))
            link(dve.tensor_copy(til, tmp.bitcast(I32)))
            link(dve.memset(one, 1.0))
            link(dve.tensor_tensor_scan(cum, one, til, 0.0, ALU.mult, ALU.add))
            link(dve.memset(tt_a[:, :], 0.0))
            link(dve.tensor_scalar(tt_b[:, :], iota_t[:, :], float(P), None, ALU.mult))
            for k in range(E - 1):
                link(dve.scalar_tensor_tensor(out=tt_a[:, :], in0=iota_t[:, :], scalar=cum[:, k:k + 1], in1=tt_a[:, :],
                                              op0=ALU.is_ge, op1=ALU.add))
                link(dve.tensor_scalar(last, til[:, k:k + 1], -float(P), float(REGION), ALU.mult, ALU.add))
                link(dve.tensor_scalar(tt_c[:, :], iota_t[:, :], cum[:, k:k + 1], last, ALU.is_ge, ALU.mult))
                link(dve.tensor_tensor(tt_b[:, :], tt_b[:, :], tt_c[:, :], ALU.add))
            link(dve.tensor_scalar(tt_c[:, :], tt_b[:, :], -1.0, count[:, E - 1:E], ALU.mult, ALU.add))
            link(dve.scalar_tensor_tensor(out=tt_c[:, :], in0=iota_t[:, :], scalar=cum[:, E - 1:E], in1=tt_c[:, :],
                                          op0=ALU.is_ge, op1=ALU.mult))
            link(dve.tensor_tensor(tt_b[:, :], tt_b[:, :], tt_c[:, :], ALU.add))
            link(dve.tensor_copy(table_row[0:1, :], tt_b[0:1, :]))
            link(dve.tensor_copy(table_e[0:1, :], tt_a[0:1, :]))
            dve.sem_inc(s_tab, 1)
            dve.tensor_tensor(gate[:, 0, :], top_all[:, :, 1], top_all[:, :, 0], ALU.subtract).then_inc(s_d, 1)
            dve.wait_ge(s_ge, 1)
            link(dve.tensor_scalar(gate[:, 0, :], gate[:, 1, :], 1.0, None, ALU.add))
            link(dve.reciprocal(gate[:, 0, :], gate[:, 0, :]))
            link(dve.tensor_tensor(gate[:, 1, :], gate[:, 1, :], gate[:, 0, :], ALU.mult))
            end = POST0 + T * POST + n[0]
            for u in range(2):
                dve.wait_ge(s_sc[u], 32 * TO)
            dve.wait_ge(s_b2, 16)

            def split_x(u, t, ringed=True):
                dve.wait_ge(s_xg, t + 1)
                if ringed:
                    dve.wait_ge(s_g1, t - 1)
                dve.tensor_copy(x_hi[u][:, :], xg[:, :]).then_inc(s_xc, 1)
                dve.wait_ge(s_xc, t + 1)
                dve.tensor_tensor(x_lo[u][:, :], xg[:, :], x_hi[u][:, :], ALU.subtract).then_inc(s_xh, 1)

            def split_h(u, t, ringed=True):
                dve.wait_ge(s_ge1, t + 1)
                if ringed:
                    dve.wait_ge(s_g2, t - 1)
                dve.tensor_copy(h_hi[u][:, :], hf[u][:, :]).then_inc(s_hc, 1)
                dve.wait_ge(s_hc, t + 1)
                dve.tensor_tensor(h_lo[u][:, :], hf[u][:, :], h_hi[u][:, :], ALU.subtract).then_inc(s_hh, 1)

            def result(o, u, t, ringed=True):
                e = dve.value_load(table_e[0:1, bass.ds(t, 1)], min_val=0, max_val=E - 1)
                dve.wait_ge(s_g2, t + 1)
                if ringed:
                    dve.wait_ge(s_ysc[u], 16 * o)
                dve.scalar_tensor_tensor(out=y_sb[u][:, :], in0=acc[u][:, 0:D], scalar=1.0 / WSCALE,
                                         in1=b2_rep[:, bass.ds(e * D, D)], op0=ALU.mult, op1=ALU.add).then_inc(s_yc, 1)
                dve.wait_ge(s_yc, t + 1)
                dve.scalar_tensor_tensor(out=y_sb[u][:, :], in0=acc[u][:, D:2 * D], scalar=1.0 / WSCALE,
                                         in1=y_sb[u][:, :], op0=ALU.mult, op1=ALU.add).then_inc(s_y, 1)

            split_x(0, 0, False)
            split_x(1, 1, False)
            split_h(0, 0, False)
            split_x(0, 2)
            split_h(1, 1, False)
            result(0, 0, 0, False)
            split_x(1, 3)
            split_h(0, 2)
            result(0, 1, 1, False)
            with dve.Fori(1, FO - 1) as o:
                split_x(0, 2 * o + 2)
                split_h(1, 2 * o + 1)
                result(o, 0, 2 * o)
                split_x(1, 2 * o + 3)
                split_h(0, 2 * o + 2)
                result(o, 1, 2 * o + 1)
            split_x(0, FT - 1)
            split_h(1, FT - 2)
            result(FO - 1, 0, FT - 3)
            split_h(0, FT - 1)
            result(FO - 1, 1, FT - 2)
            result(FO, 0, FT - 1)

            def combine(o, u):
                i = 2 * o + u
                dve.wait_ge(s_yb[u], 16 * (o + 1))
                for k in range(2):
                    for r in range(2):
                        xi = x_all[:, bass.ds(2 * i + r, 1), :].rearrange("p a d -> p (a d)")
                        ins = dve.scalar_tensor_tensor(out=xi, in0=yb[u][:, r, k * D:(k + 1) * D],
                                                       scalar=gate[:, k, bass.ds(2 * i + r, 1)], in1=xi,
                                                       op0=ALU.mult, op1=ALU.add)
                        if k == 0 and r == 1:
                            ins.then_inc(s_cb, 1)
                            dve.wait_ge(s_cb, i + 1)
                ins.then_inc(s_fin, 1)

            with dve.Fori(0, T // 4) as o:
                combine(o, 0)
                combine(o, 1)


_INS = ["x", "adj", "L0_gnn_W", "L0_gnn_a", "L0_ffn_Wr", "L0_ffn_br", "L0_ffn_ln_g", "L0_ffn_ln_b",
        "L0_ffn_W1", "L0_ffn_b1", "L0_ffn_W2", "L0_ffn_b2"]


def kernel(**inputs):
    import numpy as _np
    import concourse.bacc as _bacc
    from concourse import mybir as _mybir
    from concourse.bass_utils import run_bass_kernel_spmd as _run

    nc = _bacc.Bacc("TRN2", target_bir_lowering=False, num_devices=1)
    arrays, args = {}, []
    for name in _INS:
        a = _np.ascontiguousarray(inputs[name])
        arrays[f"in_{name}"] = a
        args.append(nc.dram_tensor(f"in_{name}", a.shape, _mybir.dt.from_np(a.dtype), kind="ExternalInput").ap())
    shape = inputs["x"].shape
    args.append(nc.dram_tensor("out_0", shape, _mybir.dt.float32, kind="ExternalOutput").ap())
    build(nc, *args)
    r = _run(nc, [arrays], core_ids=[0])
    return r.results[0]["out_0"]
```

```python
from contextlib import ExitStack

import concourse.bass as bass
from concourse import mybir

ALU = mybir.AluOpType
ACT = mybir.ActivationFunctionType
F32 = mybir.dt.float32
F16 = mybir.dt.float16
BF16 = mybir.dt.bfloat16
U32 = mybir.dt.uint32
I32 = mybir.dt.int32

P = 128
SLOPE = 0.2
LN_EPS = 1e-5
MASKED = 1.0e15
LOSCALE = 1024.0
PSCALE = 1024.0


def build(nc, x, adj, gnn_w, gnn_a, w_r, b_r, ln_g, ln_b, w1, b1, w2, b2, out):
    N, D = x.shape
    E = w_r.shape[1]
    HID = w1.shape[2]
    T = N // P
    KD = D // P
    HC = HID // P
    G = 4
    GJ = T // G
    GW = GJ * P
    HALF = N // 2
    S = 2
    R = S * P
    REGION = N + R
    ROW = D + 1
    CHUNKS = 4
    CW = KD * HID // 2
    XC = 4
    TC = T // XC
    YC = 8
    YT = T // YC
    FT = 2 * N // R + E - 1
    assert D == 256 and HID == 1024 and E == 8 and CW == 1024 and T % 4 == 0 and FT % 2 == 1

    rows_dram = nc.dram_tensor("rows_dram", [E * REGION, ROW], F32, kind="Internal").ap()
    wsplit_dram = nc.dram_tensor("wsplit_dram", [E * CHUNKS, P, 2 * CW], F16, kind="Internal").ap()
    y_dram = nc.dram_tensor("y_dram", [2 * N + FT * R, D], F32, kind="Internal").ap()

    adj_tiles = adj.rearrange("(t p) n -> t p n", p=P)
    x_view = x.rearrange("(t p) d -> p t d", p=P)
    out_view = out.rearrange("(t p) d -> p t d", p=P)
    w1_view = w1.rearrange("e (k p) h -> e k p h", p=P)
    w2_view = w2.rearrange("e (q c p) d -> e q p c d", q=2, p=P)
    y_view = y_dram[0:2 * N, :].rearrange("(t p k) d -> p t (k d)", p=P, k=2)

    with ExitStack() as ctx:
        def sb(name, shape, dt, stack=ctx):
            return stack.enter_context(nc.sbuf_tensor(name, shape, dt))

        def sem(name):
            return ctx.enter_context(nc.semaphore(name))

        def row_like(buffer, start, width):
            return buffer[:, start:start + width]

        tp = [ctx.enter_context(nc.psum_tensor(f"tp{u}", [P, GW], F32)) for u in range(2)]
        acc = [ctx.enter_context(nc.psum_tensor(f"acc{u}", [P, 2 * D], F32)) for u in range(2)]
        xt_ps = ctx.enter_context(nc.psum_tensor("xt_ps", [P, 512], F32))
        rt_ps = ctx.enter_context(nc.psum_tensor("rt_ps", [P, 512], F32))

        x_all = sb("x_all", [P, T, D], F32)
        ident = sb("ident", [P, P], F32)
        top_all = sb("top_all", [P, T, 2], F32)
        gate = sb("gate", [P, 2, T], F32)
        count = sb("count", [P, E], F32)
        table_e = sb("table_e", [1, FT], I32)
        table_row = sb("table_row", [1, FT], I32)
        tail_row = sb("tail_row", [1, E], I32)
        g_cols = sb("g_cols", [P, E, KD], F32)
        b_cols = sb("b_cols", [P, E, KD], F32)
        b1_cols = sb("b1_cols", [P, E, HC], F32)

        front = ExitStack()
        adj_sb = sb("adj_sb", [P, N], F32, front)
        bias_sb = sb("bias_sb", [P, N], BF16, front)
        t_row = sb("t_row", [P, N], F32, front)
        t2_row = sb("t2_row", [P, N], F32, front)
        sc = [sb(f"sc{u}", [P, N], F32, front) for u in range(2)]
        wh = sb("wh", [P, T, 2, D], F16, front)
        pt_hi = [sb(f"pt_hi{g}", [P, GW], F16, front) for g in range(G)]
        pt_lo = [sb(f"pt_lo{g}", [P, GW], F16, front) for g in range(G)]
        wf = [sb(f"wf{u}", [P, CW], F32, front) for u in range(2)]
        wsp = [sb(f"wsp{u}", [P, 2 * CW], F16, front) for u in range(2)]
        xn = [sb(f"xn{u}", [P, D], F32, front) for u in range(2)]
        xnt = [sb(f"xnt{u}", [P, D], F32, front) for u in range(2)]
        row_a = [sb(f"row_a{u}", [P, ROW], F32, front) for u in range(2)]
        row_b = [sb(f"row_b{u}", [P, ROW], F32, front) for u in range(2)]
        w_r_sb = sb("w_r_sb", [P, KD, E], F32, front)
        b_r_rep = sb("b_r_rep", [P, E], F32, front)
        s_col8 = sb("s_col8", [P, T], F32, front)
        half_neg = sb("half_neg", [P, T], F32, front)
        big = sb("big", [P, 1], F32, front)
        mx = sb("mx", [P, 2], F32, front)
        neg_m = [sb(f"neg_m{u}", [P, 1], F32, front) for u in range(2)]
        rsum = [sb(f"rsum{u}", [P, 2], F32, front) for u in range(2)]
        rinv = sb("rinv", [P, 2], F32, front)
        mv1 = sb("mv1", [P, 2], F32, front)
        mv2 = sb("mv2", [P, 2], F32, front)
        rs1 = sb("rs1", [P, 2], F32, front)
        rs2 = sb("rs2", [P, 2], F32, front)
        bs1 = sb("bs1", [P, 6], F32, front)
        bs2 = sb("bs2", [P, 6], F32, front)
        dest = sb("dest", [P, T, 2], F32, front)
        tri = sb("tri", [P, P], BF16, front)
        ones = sb("ones", [P, P], BF16, front)
        off_diag = sb("off_diag", [P, P], BF16, front)
        iota_e = sb("iota_e", [P, E], F32, front)
        lg = sb("lg", [P, E], F32, front)
        top8 = sb("top8", [P, 8], F32, front)
        idx8 = sb("idx8", [P, 8], U32, front)
        idxf = sb("idxf", [P, 2], F32, front)
        oh1 = sb("oh1", [P, E], F32, front)
        oh2 = sb("oh2", [P, E], F32, front)
        oh = sb("oh", [P, E], BF16, front)
        posb = sb("posb", [P, E], F32, front)
        junk = [sb(f"junk{k}", [P, E], F32, front) for k in range(2)]
        slotf = sb("slotf", [P, 2], F32, front)
        slot = [sb(f"slot{u}", [P, 2], U32, front) for u in range(2)]
        wcat = row_like(sc[1], 0, KD * (D + 2)).rearrange("p (k n) -> p k n", k=KD)
        a_rep = row_like(sc[1], 1024, 2 * D).rearrange("p (k n) -> p k n", k=2)
        wa_rep = row_like(sc[1], 1536, KD * P).rearrange("p (k n) -> p k n", k=KD)
        bst = row_like(sc[1], 2048, T * 6).rearrange("p (t n) -> p t n", t=T)
        mean, var, rstd, s_col, gap = (row_like(sc[1], 2560 + T * k, T) for k in range(5))
        wjunk = row_like(sc[1], 3072, D)
        zrow = sb("zrow", [P, S * ROW], F32, front)
        tb = sb("tb", [1, 3 * E * FT], F32, front)
        iota_t = sb("iota_t", [1, FT], F32, front)
        small = sb("small", [P, 5 * E], F32, front)
        front.close()

        ffn_stack = ExitStack()
        w_sb = sb("w_sb", [P, E * CHUNKS * 2 * CW], F16, ffn_stack)
        w_blocks = w_sb[:, :].rearrange("p (b z n) -> p b z n", z=2, n=CW)
        b2_rep = sb("b2_rep", [P, E * D], F32, ffn_stack)
        xs = [sb(f"xs{u}", [P, S, ROW], F32, ffn_stack) for u in range(2)]
        xg = sb("xg", [P, KD * R], F32, ffn_stack)
        x_hi = sb("x_hi", [P, KD * R], F16, ffn_stack)
        x_lo = sb("x_lo", [P, KD * R], F16, ffn_stack)
        x_down = sb("x_down", [P, KD * R], F16, ffn_stack)
        hf = sb("hf", [P, HC * R], F32, ffn_stack)
        h_hi = [sb(f"h_hi{u}", [P, HC * R], F16, ffn_stack) for u in range(2)]
        h_lo = [sb(f"h_lo{u}", [P, HC * R], F16, ffn_stack) for u in range(2)]
        y_sb = sb("y_sb", [P, S, D], F32, ffn_stack)
        dump = sb("dump", [P, S], F32, ffn_stack)
        dz = sb("dz", [P, S], F32, ffn_stack)
        yidx = [sb(f"yidx{u}", [P, S], U32, ffn_stack) for u in range(2)]
        ffn_stack.close()
        y_all = sb("y_all", [P, T, 2 * D], F32)

        s_sx = sem("s_col_copied")
        s_top = sem("top_logits_kept")
        s_te = sem("table_of_experts_done")
        s_wp = sem("w_chunk_rest_done")
        s_ve1 = sem("ln1_var_eps_done")
        s_ve2 = sem("ln2_var_eps_done")
        s_du = sem("dump_rows_done")
        s_dz = sem("dump_choice_done")
        s_x = [sem(f"x_loaded{c}") for c in range(4)]
        s_par = sem("gnn_params_loaded")
        s_par2 = sem("ffn_params_loaded")
        s_pc = sem("pool_consts")
        s_ps = sem("pool_step")
        s_ds = sem("dve_step")
        s_apart = sem("carries_a_register_wait")
        s_st = sem("ln_stats_done")
        s_var = sem("ln_var_done")
        s_rstd = sem("rstd_done")
        s_xn = sem("xn_done")
        s_xnt_ps = sem("xnt_in_psum")
        s_xnt = sem("xnt_in_sbuf")
        s_wa = sem("wa_done")
        s_wh = sem("wh_in_psum")
        s_whh = sem("wh_hi_done")
        s_whl = sem("wh_lo_done")
        s_tr = sem("t_row_part_done")
        s_s8 = sem("s_cols_done")
        s_adj = [sem(f"adj_half_loaded{h}") for h in range(2)]
        s_mk = [sem(f"mask_half_done{h}") for h in range(2)]
        s_relu = sem("relu_branch_done")
        s_add = sem("pool_scores_done")
        s_c = sem("dve_scores_done")
        s_dg = sem("diagonal_unmasked")
        s_b = [sem(f"masked_half_done{h}") for h in range(2)]
        s_m = sem("neg_max_done")
        s_e = [sem(f"exp_half_done{h}") for h in range(2)]
        s_t = sem("p_transposed")
        s_hi = sem("p_hi_done")
        s_lo = sem("p_lo_done")
        s_av = sem("av_done")
        s_x1 = sem("x1_step")
        s_mv1 = sem("ln1_stats")
        s_r1 = sem("ln1_rstd")
        s_xl = sem("xl_done")
        s_xlp = sem("xl_t_in_psum")
        s_xlt = sem("xl_t_in_sbuf")
        s_mv2 = sem("ln2_stats")
        s_r2 = sem("ln2_rstd")
        s_row = sem("row_done")
        s_rows = sem("both_rows_done")
        s_lg = sem("logits_done")
        s_oh = sem("onehot_done")
        s_pos = sem("positions_done")
        s_slot = sem("slots_done")
        s_top2 = sem("router_step")
        s_next = sem("next_rows_step")
        s_st2 = sem("ln2_stats_first")
        s_sc = [sem(f"rows_scattered{u}") for u in range(2)]
        s_wf = [sem(f"w_chunk_loaded{u}") for u in range(2)]
        s_wc = [sem(f"w_chunk_hi_loaded{u}") for u in range(2)]
        s_wsp = sem("w_chunk_split")
        s_wst = [sem(f"w_chunk_stored{u}") for u in range(2)]
        s_tab = sem("table_done")
        s_tail_in = sem("tail_rows_done")
        s_tail = sem("tails_zeroed")
        s_d = sem("gate_gap_done")
        s_ge = sem("gate_exp_done")
        s_wl = [sem(f"w_loaded{e}") for e in range(E)]
        s_wr = sem("w_ready_in_order")
        s_b2 = sem("b2_loaded")
        s_xs = [sem(f"xs_loaded{u}") for u in range(2)]
        s_xtp = sem("ffn_xt_in_psum")
        s_xg = sem("ffn_xt_scaled")
        s_xc = sem("ffn_x_hi_done")
        s_xh = sem("ffn_x_split")
        s_g1 = sem("ffn_hidden_half_in_psum")
        s_ge1 = sem("ffn_gelu_half_done")
        s_hc = sem("ffn_h_hi_done")
        s_hh = sem("ffn_hidden_split")
        s_g2 = sem("ffn_y_in_psum")
        s_yc = sem("ffn_y_low_added")
        s_y = sem("ffn_y_done")
        s_yi = sem("ffn_index_done")
        s_ysc = sem("y_scattered")
        s_yb = [sem(f"y_back{c}") for c in range(YC)]
        s_cb = sem("first_choice_added")
        s_fin = sem("final_done")
        s_out = sem("out_stored")

        block = ctx.enter_context(nc.Block())

        def chain(eng, sem_, base):
            n = [0]

            def link(ins):
                n[0] += 1
                ins.then_inc(sem_, 1)
                eng.wait_ge(sem_, base + n[0])
            return link, n

        X1 = 5
        TOP = 5

        def apart(eng):
            eng.sem_inc(s_apart, 1)

        def within(i, first, last):
            return not isinstance(i, int) or first <= i <= last

        TO = T // 2

        def steps(eng, body, stops={}):
            for i in range(4):
                body(i, i % 2)
            edges = sorted({4, T - 2} | set(stops))
            for a, b in zip(edges, edges[1:]):
                if a in stops:
                    stops[a]()
                with eng.Fori(a // 2, b // 2) as o:
                    body(2 * o, 0)
                    body(2 * o + 1, 1)
            for i in range(T - 2, T + 2):
                body(i, i % 2)

        @block.sync
        def _(sp):
            sp.dma_start(wcat[:, :, 0:D], gnn_w.rearrange("(k p) n -> p k n", p=P)).then_inc(s_par, 16)
            sp.dma_start(a_rep[:, :, :], gnn_a.rearrange("(o k d) -> o k d", o=1, k=2).broadcast_to([P, 2, D])).then_inc(s_par, 16)
            for c in range(XC):
                sp.dma_start(x_all[:, c * TC:(c + 1) * TC, :], x_view[:, c * TC:(c + 1) * TC, :]).then_inc(s_x[c], 16)

            def load_adj(i, h):
                sp.dma_start(adj_sb[:, h * HALF:(h + 1) * HALF], adj_tiles[i, :, h * HALF:(h + 1) * HALF]).then_inc(s_adj[h], 16)

            def load_w(e, q):
                src = w1_view[e, q] if q < 2 else w2_view[e, q - 2]
                dst = wf[q % 2][:, :]
                if q >= 2:
                    dst = dst.rearrange("p (c d) -> p c d", d=D)
                sp.dma_start(dst, src).then_inc(s_wf[q % 2], 16)

            def store_w(e, q):
                sp.wait_ge(s_wsp, CHUNKS * e + q + 1)
                sp.dma_start(wsplit_dram[CHUNKS * e + q], wsp[q % 2][:, :]).then_inc(s_wst[q % 2], 16)

            load_adj(0, 0)
            load_adj(0, 1)
            with nc.allow_non_contiguous_dma(reason="one column for each partition"):
                sp.dma_start(g_cols[:, :, :], ln_g.rearrange("e (k p) -> p e k", p=P)).then_inc(s_par2, 16)
                sp.dma_start(b_cols[:, :, :], ln_b.rearrange("e (k p) -> p e k", p=P)).then_inc(s_par2, 16)
                sp.dma_start(b1_cols[:, :, :], b1.rearrange("e (c p) -> p e c", p=P)).then_inc(s_par2, 16)
            sp.dma_start(w_r_sb[:, :, :], w_r.rearrange("(k p) e -> p k e", p=P)).then_inc(s_par2, 16)
            sp.dma_start(b_r_rep[:, :], b_r.rearrange("(o e) -> o e", o=1).broadcast_to([P, E])).then_inc(s_par2, 16)

            def tile_step(e, first=False, last=False):
                for q in range(CHUNKS):
                    i = CHUNKS * e + q
                    for h in range(2):
                        if not (last and q == CHUNKS - 1):
                            sp.wait_ge(s_mk[h], i + 1)
                            load_adj(i + 1, h)
                    if not (first and q < 2):
                        sp.wait_ge(s_wsp, i - 1)
                    load_w(e, q)
                    if q >= 1:
                        store_w(e, q - 1)
                    elif not first:
                        store_w(e - 1, CHUNKS - 1)

            tile_step(0, first=True)
            with sp.Fori(1, E - 1) as e:
                tile_step(e)
            tile_step(E - 1, last=True)
            store_w(E - 1, CHUNKS - 1)
            for u in range(2):
                sp.wait_ge(s_wst[u], 16 * E * CHUNKS // 2)

            def load_expert(e):
                sp.dma_start(w_sb[:, e * CHUNKS * 2 * CW:(e + 1) * CHUNKS * 2 * CW].rearrange("p (q n) -> p q n", q=CHUNKS),
                             wsplit_dram[e * CHUNKS:(e + 1) * CHUNKS].rearrange("q p n -> p q n")).then_inc(s_wl[e], 16)

            for h in range(2):
                sp.wait_ge(s_mk[h], T)
            load_expert(0)
            sp.wait_ge(s_m, T)
            sp.wait_ge(s_c, T)
            sp.wait_ge(s_relu, T)
            sp.wait_ge(s_add, 2 * T)
            load_expert(1)
            sp.wait_ge(s_tail_in, 1)
            for k in range(E):
                row = sp.value_load(tail_row[0:1, k:k + 1], min_val=0, max_val=E * REGION - R)
                sp.dma_start(rows_dram[bass.ds(row, R), :].rearrange("(s p) d -> p s d", p=P),
                             zrow[:, :].rearrange("p (s d) -> p s d", s=S)).then_inc(s_tail, 16)
            sp.wait_ge(s_tail, 16 * E)
            for u in range(2):
                sp.wait_ge(s_sc[u], 32 * TO)
            sp.wait_ge(s_av, G * T)
            sp.wait_ge(s_slot, T)
            sp.wait_ge(s_tab, 1)
            sp.wait_ge(s_d, 1)
            sp.dma_start(b2_rep[:, :], b2.rearrange("(o e) d -> o (e d)", o=1).broadcast_to([P, E * D])).then_inc(s_b2, 16)
            for u in range(2):
                sp.wait_ge(s_xs[u], 16)
            for e in range(E):
                sp.wait_ge(s_wl[e], 16)
                sp.sem_inc(s_wr, 1)
                if e + 2 < E:
                    load_expert(e + 2)

            sp.wait_ge(s_ysc, 16 * S * FT)
            for c in range(YC):
                sp.dma_start(y_all[:, c * YT:(c + 1) * YT, :], y_view[:, c * YT:(c + 1) * YT, :]).then_inc(s_yb[c], 16)
            for c in range(YC):
                sp.wait_ge(s_fin, c + 1)
                sp.dma_start(out_view[:, c * YT:(c + 1) * YT, :], x_all[:, c * YT:(c + 1) * YT, :]).then_inc(s_out, 16)
            sp.wait_ge(s_out, 16 * YC)

        @block.gpsimd
        def _(pool):
            pool.memset(ident[:, :], 0.0).then_inc(s_ps, 1)
            pool.memset(tri[:, :], 1.0).then_inc(s_ps, 1)
            pool.memset(half_neg[:, :], -0.5).then_inc(s_ps, 1)
            pool.memset(ones[:, :], 1.0).then_inc(s_ps, 1)
            pool.memset(zrow[:, :], 0.0).then_inc(s_ps, 1)
            pool.wait_ge(s_ps, 5)
            pool.affine_select(out=ident[:, :], in_=ident[:, :], compare_op=ALU.not_equal, fill=1.0, base=0,
                               pattern=[[-1, P]], channel_multiplier=1).then_inc(s_pc, 1)
            pool.affine_select(out=tri[:, :], in_=tri[:, :], compare_op=ALU.is_gt, fill=0.0, base=0,
                               pattern=[[1, P]], channel_multiplier=-1).then_inc(s_pc, 1)
            pool.affine_select(out=off_diag[:, :], in_=ones[:, :], compare_op=ALU.not_equal, fill=0.0, base=0,
                               pattern=[[-1, P]], channel_multiplier=1).then_inc(s_pc, 1)
            pool.iota(iota_e[:, :], [[1, E]], base=0, channel_multiplier=0,
                      allow_small_or_imprecise_dtypes=True).then_inc(s_pc, 1)
            pool.iota(count[:, :], [[REGION, E]], base=0, channel_multiplier=0,
                      allow_small_or_imprecise_dtypes=True).then_inc(s_pc, 1)
            pool.iota(iota_t[:, :], [[1, FT]], base=0, channel_multiplier=0,
                      allow_small_or_imprecise_dtypes=True).then_inc(s_pc, 1)
            pool.iota(dest[:, :, :], [[2 * P, T], [1, 2]], base=1, channel_multiplier=2,
                      allow_small_or_imprecise_dtypes=True).then_inc(s_pc, 1)
            for c in range(XC):
                cols = slice(c * TC, (c + 1) * TC)
                pool.wait_ge(s_var, c + 1)
                pool.tensor_scalar(rstd[:, cols], var[:, cols], 1.0, LN_EPS, ALU.mult, ALU.add).then_inc(s_ps, 1)
                pool.wait_ge(s_ps, 6 + c)
                pool.tensor_tensor(rstd[:, cols], rstd[:, cols], half_neg[:, cols], ALU.pow).then_inc(s_rstd, 1)

            def scores(n, u, h):
                if h == 0:
                    pool.wait_ge(s_relu, n + 1)
                cols = slice(h * HALF // 2, (h + 1) * HALF // 2)
                pool.tensor_tensor(sc[u][:, cols], sc[u][:, cols], t2_row[:, cols], ALU.add).then_inc(s_add, 1)

            def cast_w(e, q):
                if not (isinstance(e, int) and e == 0 and q < 2):
                    pool.wait_ge(s_wst[q % 2], 16 * (2 * e + q // 2))
                    apart(pool)
                src = w1_view[e, q] if q < 2 else w2_view[e, q - 2]
                dst = wsp[q % 2][:, 0:CW]
                if q >= 2:
                    dst = dst.rearrange("p (c d) -> p c d", d=D)
                pool.dma_start(dst, src).then_inc(s_wc[q % 2], 16)

            def split_w(e, q):
                i = CHUNKS * e + q
                u = q % 2
                pool.wait_ge(s_wf[u], 16 * (2 * e + q // 2 + 1))
                pool.wait_ge(s_wc[u], 16 * (2 * e + q // 2 + 1))
                pool.tensor_tensor(wf[u][:, :], wf[u][:, :], wsp[u][:, 0:CW], ALU.subtract).then_inc(s_wp, 1)
                pool.wait_ge(s_wp, i + 1)
                apart(pool)
                pool.tensor_scalar(wsp[u][:, CW:2 * CW], wf[u][:, :], LOSCALE, 0.0, ALU.mult, ALU.add).then_inc(s_wsp, 1)

            def rstd1(n):
                pool.wait_ge(s_mv1, n + 1)
                apart(pool)
                pool.tensor_scalar(rs1[:, 0:1], mv1[:, 1:2], 1.0, LN_EPS, ALU.mult, ALU.add).then_inc(s_ve1, 1)
                pool.wait_ge(s_ve1, n + 1)
                pool.tensor_tensor(rs1[:, 1:2], rs1[:, 0:1], half_neg[:, 0:1], ALU.pow).then_inc(s_r1, 1)

            def rstd2(n):
                pool.wait_ge(s_mv2, n + 1)
                apart(pool)
                pool.tensor_scalar(rs2[:, 0:1], mv2[:, 1:2], 1.0, LN_EPS, ALU.mult, ALU.add).then_inc(s_ve2, 1)
                pool.wait_ge(s_ve2, n + 1)
                pool.tensor_tensor(rs2[:, 1:2], rs2[:, 0:1], half_neg[:, 0:1], ALU.pow).then_inc(s_r2, 1)

            def copy_row(n, u):
                pool.wait_ge(s_row, n + 1)
                apart(pool)
                pool.tensor_copy(row_b[u][:, 0:D], row_a[u][:, 0:D]).then_inc(s_rows, 1)
                pool.tensor_copy(row_a[u][:, D:ROW], dest[:, bass.ds(n, 1), 0]).then_inc(s_rows, 1)
                pool.tensor_copy(row_b[u][:, D:ROW], dest[:, bass.ds(n, 1), 1]).then_inc(s_rows, 1)

            def scatter_rows(n, u):
                pool.wait_ge(s_rows, 3 * n + 3)
                pool.wait_ge(s_slot, n + 1)
                apart(pool)
                for k, rows in enumerate((row_a, row_b)):
                    pool.indirect_dma_start(
                        out=rows_dram[:, :], out_offset=bass.IndirectOffsetOnAxis(ap=slot[u][:, k:k + 1], axis=0),
                        in_=rows[u][:, :], in_offset=None).then_inc(s_sc[u], 16)

            def step(e, q):
                i = CHUNKS * e + q
                u = q % 2
                if within(i, 2, T + 1):
                    copy_row(i - 2, u)
                if within(i, 3, T + 2):
                    scatter_rows(i - 3, 1 - u)
                if within(i, 0, T - 2):
                    cast_w(e + (q + 1) // CHUNKS, (q + 1) % CHUNKS)
                if within(i, 0, T - 1):
                    split_w(e, q)
                if within(i, 0, T - 3):
                    scores(i + 2, u, 0)
                if within(i, 1, T):
                    rstd1(i - 1)
                if within(i, 0, T - 3):
                    scores(i + 2, u, 1)
                if within(i, 1, T):
                    rstd2(i - 1)

            cast_w(0, 0)
            for h in range(2):
                scores(0, 0, h)
            for h in range(2):
                scores(1, 1, h)
            for q in range(CHUNKS):
                step(0, q)
            with pool.Fori(1, E - 1) as e:
                for q in range(CHUNKS):
                    step(e, q)
            for i in range(T - CHUNKS, T + 3):
                step(i // CHUNKS, i % CHUNKS)

            for u in range(2):
                pool.wait_ge(s_sc[u], 32 * TO)
            pool.wait_ge(s_av, G * T)
            pool.wait_ge(s_d, 1)
            pool.iota(dump[:, :], [[P, S]], base=2 * N + 1, channel_multiplier=1,
                      allow_small_or_imprecise_dtypes=True).then_inc(s_du, 1)

            def index(o, u):
                t = 2 * o + u
                pool.wait_ge(s_xs[u], 16 * (o + 1))
                pool.wait_ge(s_du, t + 1)
                if within(t, 1, FT):
                    pool.wait_ge(s_yi, S * t)
                for s in range(S):
                    apart(pool)
                    pool.tensor_scalar(dz[:, s:s + 1], xs[u][:, s, D:ROW], 0.0, dump[:, s:s + 1], ALU.is_equal, ALU.mult).then_inc(s_dz, 1)
                pool.wait_ge(s_dz, S * t + S)
                apart(pool)
                pool.tensor_scalar(dump[:, :], dump[:, :], 1.0, float(R), ALU.mult, ALU.add).then_inc(s_du, 1)
                if within(t, 2, FT):
                    pool.wait_ge(s_ysc, 16 * S * (t - 1))
                    apart(pool)
                for s in range(S):
                    pool.tensor_scalar(yidx[u][:, s:s + 1], xs[u][:, s, D:ROW], -1.0, dz[:, s:s + 1], ALU.add, ALU.add).then_inc(s_yi, 1)

            def scatter_y(t, u):
                pool.wait_ge(s_yi, S * t + S)
                pool.wait_ge(s_y, t + 1)
                apart(pool)
                for s in range(S):
                    pool.indirect_dma_start(
                        out=y_dram[:, :], out_offset=bass.IndirectOffsetOnAxis(ap=yidx[u][:, s:s + 1], axis=0),
                        in_=y_sb[:, s, :], in_offset=None).then_inc(s_ysc, 16)

            index(0, 0)
            index(0, 1)
            scatter_y(0, 0)
            with pool.Fori(1, FT // 2) as o:
                index(o, 0)
                scatter_y(2 * o - 1, 1)
                index(o, 1)
                scatter_y(2 * o, 0)
            index(FT // 2, 0)
            scatter_y(FT - 2, 1)
            scatter_y(FT - 1, 0)

        @block.tensor
        def _(pe):
            pe.wait_ge(s_pc, 7)

            def project_t(i, u):
                pe.wait_ge(s_xn, i + 1)
                if within(i, 2, T):
                    pe.wait_ge(s_xnt, i - 1)
                for k in range(KD):
                    m = pe.transpose(tp[u][:, k * P:(k + 1) * P], xn[u][:, k * P:(k + 1) * P], ident[:, :])
                m.then_inc(s_xnt_ps, 1)

            def project(i, u):
                pe.wait_ge(s_xnt, i + 1)
                if within(i, 2, T):
                    pe.wait_ge(s_whl, i - 1)
                    pe.wait_ge(s_tr, 2 * i - 2)
                for k in range(KD):
                    pe.matmul(tp[u][:, 512:512 + D + 2], xnt[u][:, k * P:(k + 1) * P], wcat[:, k, :],
                              start=(k == 0), stop=(k == KD - 1))
                for k in range(KD):
                    m = pe.matmul(acc[u][:, 0:P], wa_rep[:, k, :], xnt[u][:, k * P:(k + 1) * P],
                                  start=(k == 0), stop=(k == KD - 1))
                m.then_inc(s_wh, 1)

            pe.wait_ge(s_wa, 1)

            def first_step(i, u):
                if within(i, 0, T - 1):
                    project_t(i, u)
                if within(i, 1, T):
                    project(i - 1, 1 - u)

            steps(pe, first_step)

            def p_transpose(i, u, g):
                if g % 2 == 0:
                    pe.wait_ge(s_e[g // 2], i + 1)
                if within(G * i + g, 2, G * T):
                    pe.wait_ge(s_lo, G * i + g - 1)
                for c in range(GJ):
                    m = pe.transpose(tp[g % 2][:, c * P:(c + 1) * P], sc[u][:, (GJ * g + c) * P:(GJ * g + c + 1) * P], ident[:, :])
                m.then_inc(s_t, 1)

            def av(i, u, g):
                pe.wait_ge(s_lo, G * i + g + 1)
                if g == 0 and within(i, 2, T):
                    pe.wait_ge(s_x1, X1 * (i - 2) + 4)
                for c in range(GJ):
                    j = GJ * g + c
                    pe.matmul(acc[u][:, :], pt_hi[g][:, c * P:(c + 1) * P], wh[:, j, :, :],
                              start=(j == 0), stop=False, skip_group_check=True)
                    m = pe.matmul(acc[u][:, 0:D], pt_lo[g][:, c * P:(c + 1) * P], wh[:, j, 0, :],
                                  start=False, stop=(j == T - 1), skip_group_check=True)
                m.then_inc(s_av, 1)

            def router_t(i):
                pe.wait_ge(s_xl, i + 1)
                for k in range(KD):
                    m = pe.transpose(xt_ps[:, k * P:(k + 1) * P], xn[0][:, k * P:(k + 1) * P], ident[:, :])
                m.then_inc(s_xlp, 1)

            def router_mm(i):
                pe.wait_ge(s_xlt, i + 1)
                if within(i, 1, T):
                    pe.wait_ge(s_slot, i)
                for k in range(KD):
                    m = pe.matmul(rt_ps[:, 0:E], xnt[0][:, k * P:(k + 1) * P], w_r_sb[:, k, :], start=(k == 0), stop=(k == KD - 1))
                m.then_inc(s_lg, 1)

            def router_pos(i):
                pe.wait_ge(s_oh, i + 1)
                pe.matmul(rt_ps[:, 16:16 + E], tri[:, :], oh[:, :], start=True, stop=True)
                pe.matmul(rt_ps[:, 32:32 + E], ones[:, :], oh[:, :], start=True, stop=True).then_inc(s_pos, 1)

            def attend(i, u):
                now = within(i, 0, T - 1)
                if now:
                    p_transpose(i, u, 0)
                if within(i, 1, T):
                    av(i - 1, 1 - u, 3)
                if within(i, 2, T + 1):
                    router_t(i - 2)
                if now:
                    p_transpose(i, u, 1)
                    av(i, u, 0)
                if within(i, 2, T + 1):
                    router_mm(i - 2)
                if now:
                    p_transpose(i, u, 2)
                    av(i, u, 1)
                    p_transpose(i, u, 3)
                    av(i, u, 2)
                if within(i, 2, T + 1):
                    router_pos(i - 2)

            pe.wait_ge(s_whl, T)
            steps(pe, attend)

            def ffn_t(o, u):
                pe.wait_ge(s_xs[u], 16 * (o + 1))
                if within(2 * o + u, 1, FT):
                    pe.wait_ge(s_xg, 2 * o + u)
                for k in range(KD):
                    for s in range(S):
                        m = pe.transpose(xt_ps[:, k * R + s * P:k * R + (s + 1) * P], xs[u][:, s, k * P:(k + 1) * P], ident[:, :])
                m.then_inc(s_xtp, 1)

            def expert_of(t):
                return pe.value_load(table_e[0:1, bass.ds(t, 1)], min_val=0, max_val=E - 1)

            def up(t):
                e = expert_of(t)
                pe.wait_ge(s_wr, e + 1)
                pe.wait_ge(s_xh, t + 1)
                for c in range(HC):
                    if c % (HC // 2) == 0 and within(t, 1, FT):
                        pe.wait_ge(s_ge1, 2 * t - 1 + c // (HC // 2))
                    o = tp[c // 4][:, (c % 4) * R:(c % 4 + 1) * R]
                    for k in range(KD):
                        at = e * (CHUNKS * 2 * CW) + k * 2 * CW + c * P
                        w_hi = w_sb[:, bass.ds(at, P)]
                        w_lo = w_sb[:, bass.ds(at + CW, P)]
                        cols = slice(k * R, (k + 1) * R)
                        pe.matmul(o, w_hi, x_hi[:, cols], start=(k == 0), stop=False)
                        pe.matmul(o, w_hi, x_lo[:, cols], start=False, stop=False)
                        m = pe.matmul(o, w_lo, x_down[:, cols], start=False, stop=(k == KD - 1))
                    if c % (HC // 2) == HC // 2 - 1:
                        m.then_inc(s_g1, 1)

            def down(t, u):
                e = expert_of(t)
                pe.wait_ge(s_hh, t + 1)
                if within(t, 1, FT):
                    pe.wait_ge(s_y, t)
                for c in range(HC):
                    w_both = w_blocks[:, bass.ds(e * CHUNKS + 2 + c // 4, 1), :, (c % 4) * D:(c % 4 + 1) * D].rearrange("p a z n -> p (a z) n")
                    w_hi = w_both[:, 0, :]
                    for s in range(S):
                        pe.matmul(acc[s][:, :], h_hi[u][:, c * R + s * P:c * R + (s + 1) * P], w_both,
                                  start=(c == 0), stop=False, skip_group_check=True)
                    for s in range(S):
                        m = pe.matmul(acc[s][:, 0:D], h_lo[u][:, c * R + s * P:c * R + (s + 1) * P], w_hi,
                                      start=False, stop=(c == HC - 1), skip_group_check=True)
                m.then_inc(s_g2, 1)

            pe.wait_ge(s_tab, 1)
            for u in range(2):
                pe.wait_ge(s_sc[u], 32 * TO)
            ffn_t(0, 0)
            up(0)
            ffn_t(0, 1)

            def pair(o):
                up(2 * o + 1)
                ffn_t(o + 1, 0)
                down(2 * o, 0)
                up(2 * o + 2)
                ffn_t(o + 1, 1)
                down(2 * o + 1, 1)

            pair(0)
            with pe.Fori(1, FT // 2 - 1) as o:
                pair(o)
            up(FT - 2)
            ffn_t(FT // 2, 0)
            down(FT - 3, 0)
            up(FT - 1)
            down(FT - 2, 1)
            down(FT - 1, 0)

        @block.scalar
        def _(act):
            def mask(n, h):
                act.wait_ge(s_adj[h], 16 * (n + 1))
                if within(n, 1, T):
                    act.wait_ge(s_b[h], n)
                cols = slice(h * HALF, (h + 1) * HALF)
                act.activation(bias_sb[:, cols], adj_sb[:, cols], ACT.Relu, bias=big[:, 0:1], scale=-3.0e38).then_inc(s_mk[h], 1)

            def first_step(i, u):
                if within(i, 0, T - 1):
                    act.wait_ge(s_xnt_ps, i + 1)
                    if within(i, 2, T):
                        act.wait_ge(s_wh, i - 1)
                    act.activation(xnt[u][:, :], tp[u][:, 0:D], ACT.Copy).then_inc(s_xnt, 1)
                if within(i, 1, T):
                    n, v = i - 1, 1 - u
                    act.wait_ge(s_wh, n + 1)
                    act.activation(wh[:, bass.ds(n, 1), 0, :], tp[v][:, 512:512 + D], ACT.Copy).then_inc(s_whh, 1)
                    act.activation(t_row[:, bass.ds(n * P, P)], acc[v][:, 0:P], ACT.Copy).then_inc(s_tr, 1)
                    act.activation(t2_row[:, bass.ds(n * P, P)], acc[v][:, 0:P], ACT.Copy, scale=SLOPE).then_inc(s_tr, 1)

            act.wait_ge(s_ds, 1)
            steps(act, first_step, {T // 2: lambda: [mask(0, h) for h in range(2)]})

            def relu_branch(n, u):
                if within(n, 2, T):
                    act.wait_ge(s_t, G * (n - 2) + 2)
                act.activation(sc[u][:, 0:HALF], t_row[:, 0:HALF], ACT.Relu, bias=s_col8[:, bass.ds(n, 1)],
                               scale=1.0 - SLOPE).then_inc(s_relu, 1)

            def exps(n, u, h):
                if h == 0:
                    act.wait_ge(s_m, n + 1)
                cols = slice(h * HALF, (h + 1) * HALF)
                act.activation(sc[u][:, cols], sc[u][:, cols], ACT.Exp, bias=neg_m[u][:, 0:1], scale=1.0,
                               accum_out=rsum[u][:, h:h + 1]).then_inc(s_e[h], 1)

            def p_hi(i, g):
                act.wait_ge(s_t, G * i + g + 1)
                if within(i, 1, T):
                    act.wait_ge(s_av, G * i + g - 3)
                act.activation(pt_hi[g][:, :], tp[g % 2][:, :], ACT.Copy, scale=PSCALE).then_inc(s_hi, 1)

            def router(n):
                act.wait_ge(s_xlp, n + 1)
                act.activation(xnt[0][:, :], xt_ps[:, 0:D], ACT.Copy).then_inc(s_xlt, 1)

            def attend(i, u):
                now = within(i, 0, T - 1)
                ahead = within(i, 0, T - 3)
                if now:
                    p_hi(i, 0)
                    exps(i, u, 1)
                if within(i, 2, T + 1):
                    router(i - 2)
                if now:
                    p_hi(i, 1)
                if ahead:
                    relu_branch(i + 2, u)
                if now:
                    p_hi(i, 2)
                if ahead:
                    mask(i + 2, 0)
                if within(i, 0, T - 2):
                    exps(i + 1, 1 - u, 0)
                if now:
                    p_hi(i, 3)
                if ahead:
                    mask(i + 2, 1)

            act.wait_ge(s_s8, 2)
            act.wait_ge(s_tr, 2 * T)
            relu_branch(0, 0)
            relu_branch(1, 1)
            mask(1, 0)
            exps(0, 0, 0)
            mask(1, 1)
            steps(act, attend)
            act.wait_ge(s_d, 1)
            act.activation(gate[:, 1, :], gate[:, 0, :], ACT.Exp).then_inc(s_ge, 1)

            def load_x(o, u):
                if within(o, 1, FT):
                    act.wait_ge(s_yi, S * (2 * o + u - 1))
                row = act.value_load(table_row[0:1, bass.ds(2 * o + u, 1)], min_val=0, max_val=E * REGION - R)
                act.dma_start(xs[u][:, :, :], rows_dram[bass.ds(row, R), :].rearrange("(s p) d -> p s d", p=P)).then_inc(s_xs[u], 16)

            def expert_of(t):
                return act.value_load(table_e[0:1, bass.ds(t, 1)], min_val=0, max_val=E - 1)

            def scaled(t):
                e = expert_of(t)
                act.wait_ge(s_xtp, t + 1)
                if within(t, 1, FT):
                    act.wait_ge(s_xh, t)
                for k in range(KD):
                    ins = act.activation(xg[:, k * R:(k + 1) * R], xt_ps[:, k * R:(k + 1) * R], ACT.Identity,
                                         bias=b_cols[:, bass.ds(e, 1), k], scale=g_cols[:, bass.ds(e, 1), k])
                ins.then_inc(s_xg, 1)

            def gelu(t):
                e = expert_of(t)
                for c in range(HC):
                    if c % (HC // 2) == 0:
                        act.wait_ge(s_g1, 2 * t + 1 + c // (HC // 2))
                        if c == 0 and within(t, 1, FT):
                            act.wait_ge(s_hh, t)
                    ins = act.activation(hf[:, c * R:(c + 1) * R], tp[c // 4][:, (c % 4) * R:(c % 4 + 1) * R], ACT.Gelu,
                                         bias=b1_cols[:, bass.ds(e, 1), c])
                    if c % (HC // 2) == HC // 2 - 1:
                        ins.then_inc(s_ge1, 1)

            act.wait_ge(s_tab, 1)
            for u in range(2):
                act.wait_ge(s_sc[u], 32 * TO)
            act.wait_ge(s_tail, 16 * E)
            act.wait_ge(s_av, G * T)
            load_x(0, 0)
            load_x(0, 1)
            scaled(0)

            def pair(o, last=False):
                scaled(2 * o + 1)
                gelu(2 * o)
                load_x(o + 1, 0)
                scaled(2 * o + 2)
                gelu(2 * o + 1)
                if not last:
                    load_x(o + 1, 1)

            pair(0)
            with act.Fori(1, FT // 2 - 1) as o:
                pair(o)
            pair(FT // 2 - 1, last=True)
            gelu(FT - 1)

        @block.vector
        def _(dve):
            def tile_of(i):
                return x_all[:, bass.ds(i, 1), :].rearrange("p a d -> p (a d)")

            link, n = chain(dve, s_ds, 0)
            link(dve.memset(big[:, :], MASKED))
            dve.wait_ge(s_par, 16 * 2)
            dve.wait_ge(s_pc, 7)
            for k in range(KD):
                for h in range(2):
                    link(dve.tensor_tensor_reduce(wjunk, wcat[:, k, 0:D], a_rep[:, h, :], 1.0, 0.0,
                                                  ALU.mult, ALU.add, wcat[:, k, D + h:D + h + 1]))
            for k in range(KD):
                ins = dve.tensor_scalar(wa_rep[:, k, :], ones[:, :], wcat[:, k, D + 1:D + 2], None, ALU.mult)
            ins.then_inc(s_wa, 1)

            def moments(c):
                dve.wait_ge(s_x[c], 16)
                for i in range(c * TC, (c + 1) * TC):
                    ins = dve.bn_stats(bst[:, i, :], x_all[:, i, :])
                link(ins)
                m, v, g = (buffer[:, c * TC:(c + 1) * TC] for buffer in (mean, var, gap))
                b = bst[:, c * TC:(c + 1) * TC, :]
                dve.tensor_tensor(m, b[:, :, 1], b[:, :, 4], ALU.add)
                dve.tensor_tensor(g, b[:, :, 1], b[:, :, 4], ALU.subtract)
                link(dve.tensor_tensor(v, b[:, :, 2], b[:, :, 5], ALU.add))
                link(dve.scalar_tensor_tensor(out=g, in0=g, scalar=D / 4.0, in1=g, op0=ALU.mult, op1=ALU.mult))
                link(dve.tensor_tensor(v, v, g, ALU.add))
                dve.tensor_scalar(v, v, 1.0 / D, None, ALU.mult).then_inc(s_var, 1)
                link(dve.tensor_scalar(m, m, 0.5, None, ALU.mult))

            def first_step(i, u):
                if within(i, 0, T - 1):
                    if within(i, 2, T):
                        dve.wait_ge(s_xnt_ps, i - 1)
                    dve.tensor_scalar(xn[u][:, :], tile_of(i), mean[:, bass.ds(i, 1)], rstd[:, bass.ds(i, 1)],
                                      ALU.subtract, ALU.mult).then_inc(s_xn, 1)
                if within(i, 2, T + 1):
                    n = i - 2
                    dve.wait_ge(s_whh, n + 1)
                    dve.tensor_copy(s_col[:, bass.ds(n, 1)], tp[u][:, 512 + D:512 + D + 1]).then_inc(s_sx, 1)
                    dve.tensor_tensor(wh[:, bass.ds(n, 1), 1, :], tp[u][:, 512:512 + D], wh[:, bass.ds(n, 1), 0, :],
                                      ALU.subtract).then_inc(s_whl, 1)

            def next_moments(c):
                dve.wait_ge(s_rstd, c)
                if c < XC:
                    moments(c)

            moments(0)
            next_moments(1)
            dve.wait_ge(s_wa, 1)
            steps(dve, first_step, {(c - 2) * TC + 4: lambda c=c: next_moments(c) for c in range(2, XC + 1)})
            base = n[0]
            dve.wait_ge(s_whl, T)
            dve.wait_ge(s_sx, T)
            dve.tensor_scalar(s_col8[:, :], s_col, 1.0 - SLOPE, None, ALU.mult).then_inc(s_s8, 1)
            dve.wait_ge(s_s8, 1)
            dve.wait_ge(s_wh, T)
            dve.wait_ge(s_par2, 16 * 5)
            dve.sem_inc(s_s8, 1)
            dve.wait_ge(s_tr, 2 * T)

            def scores(n, u):
                if within(n, 2, T):
                    dve.wait_ge(s_t, G * (n - 1))
                dve.scalar_tensor_tensor(out=sc[u][:, HALF:N], in0=t_row[:, HALF:N], scalar=s_col8[:, bass.ds(n, 1)],
                                         in1=t2_row[:, HALF:N], op0=ALU.add, op1=ALU.max).then_inc(s_c, 1)

            def diagonal(n):
                for k in range(2):
                    dve.wait_ge(s_mk[k], n + 1)
                diag = bias_sb[:, bass.ds(n * P, P)]
                dve.tensor_tensor(diag, diag, off_diag[:, :], ALU.mult).then_inc(s_dg, 1)

            def masked(n, u, h):
                if h == 0:
                    dve.wait_ge(s_add, 2 * n + 2)
                    dve.wait_ge(s_c, n + 1)
                    dve.wait_ge(s_dg, n + 1)
                    apart(dve)
                cols = slice(h * HALF, (h + 1) * HALF)
                dve.tensor_tensor_reduce(sc[u][:, cols], sc[u][:, cols], bias_sb[:, cols], 1.0, -3.0e38,
                                         ALU.subtract, ALU.max, mx[:, h:h + 1]).then_inc(s_b[h], 1)

            def negated_max(n, u):
                for k in range(2):
                    dve.wait_ge(s_b[k], n + 1)
                dve.tensor_scalar(neg_m[u][:, :], mx[:, 0:1], mx[:, 1:2], -1.0, ALU.max, ALU.mult).then_inc(s_m, 1)

            def p_lo(i, g):
                dve.wait_ge(s_hi, G * i + g + 1)
                dve.scalar_tensor_tensor(out=pt_lo[g][:, :], in0=tp[g % 2][:, :], scalar=PSCALE, in1=pt_hi[g][:, :],
                                         op0=ALU.mult, op1=ALU.subtract).then_inc(s_lo, 1)

            def row_sum(n, u):
                dve.wait_ge(s_av, G * n + G)
                dve.wait_ge(s_e[1], n + 1)
                dve.tensor_scalar(rinv[:, 0:1], rsum[u][:, 0:1], rsum[u][:, 1:2], PSCALE, ALU.add, ALU.mult).then_inc(s_x1, 1)

            def row_reciprocal(n):
                dve.wait_ge(s_x1, X1 * n + 1)
                dve.reciprocal(rinv[:, 1:2], rinv[:, 0:1]).then_inc(s_x1, 1)

            def add_attention(n, u, h):
                dve.wait_ge(s_x1, X1 * n + 2 + h)
                dve.scalar_tensor_tensor(out=tile_of(n), in0=acc[u][:, h * D:(h + 1) * D], scalar=rinv[:, 1:2], in1=tile_of(n),
                                         op0=ALU.mult, op1=ALU.add).then_inc(s_x1, 1)

            def stats1(n):
                dve.wait_ge(s_x1, X1 * n + 4)
                apart(dve)
                dve.bn_stats(bs1[:, :], tile_of(n)).then_inc(s_x1, 1)

            def moments1(n):
                dve.wait_ge(s_x1, X1 * n + 5)
                if within(n, 1, T):
                    dve.wait_ge(s_r1, n)
                apart(dve)
                dve.bn_aggr(mv1[:, :], bs1[:, :]).then_inc(s_mv1, 1)

            def normalise1(n):
                dve.wait_ge(s_r1, n + 1)
                dve.wait_ge(s_mv1, n + 1)
                if within(n, 1, T):
                    dve.wait_ge(s_xlp, n)
                dve.tensor_scalar(xn[0][:, :], tile_of(n), mv1[:, 0:1], rs1[:, 1:2], ALU.subtract, ALU.mult).then_inc(s_xl, 1)

            def stats2(n):
                dve.wait_ge(s_xl, n + 1)
                apart(dve)
                dve.bn_stats(bs2[:, :], xn[0][:, :]).then_inc(s_st2, 1)

            def moments2(n):
                dve.wait_ge(s_st2, n + 1)
                if within(n, 1, T):
                    dve.wait_ge(s_r2, n)
                apart(dve)
                dve.bn_aggr(mv2[:, :], bs2[:, :]).then_inc(s_mv2, 1)

            def normalise2(n, u):
                dve.wait_ge(s_r2, n + 1)
                dve.wait_ge(s_mv2, n + 1)
                if within(n, 2, T):
                    dve.wait_ge(s_sc[u], 16 * (n - u))
                dve.tensor_scalar(row_a[u][:, 0:D], xn[0][:, :], mv2[:, 0:1], rs2[:, 1:2], ALU.subtract,
                                  ALU.mult).then_inc(s_row, 1)

            def logits(n):
                dve.wait_ge(s_lg, n + 1)
                dve.tensor_tensor(lg[:, :], rt_ps[:, 0:E], b_r_rep[:, :], ALU.add).then_inc(s_top2, 1)

            def largest(n):
                dve.wait_ge(s_top2, TOP * n + 1)
                apart(dve)
                dve.max(top8[:, :], lg[:, :]).then_inc(s_top2, 1)

            def experts(n):
                dve.wait_ge(s_top2, TOP * n + 2)
                apart(dve)
                dve.max_index(idx8[:, :], top8[:, :], lg[:, :]).then_inc(s_top2, 1)

            def keep_top(n):
                dve.tensor_copy(top_all[:, bass.ds(n, 1), :].rearrange("p a d -> p (a d)"), top8[:, 0:2]).then_inc(s_top, 1)
                dve.wait_ge(s_top2, TOP * n + 3)
                dve.tensor_copy(idxf[:, :], idx8[:, 0:2]).then_inc(s_top2, 1)

            def one_hots(n):
                dve.wait_ge(s_top2, TOP * n + 4)
                dve.tensor_scalar(oh1[:, :], iota_e[:, :], idxf[:, 0:1], None, ALU.is_equal)
                dve.tensor_scalar(oh2[:, :], iota_e[:, :], idxf[:, 1:2], None, ALU.is_equal).then_inc(s_top2, 1)

            def both_hots(n):
                dve.wait_ge(s_top2, TOP * n + 5)
                dve.tensor_tensor(oh[:, :], oh1[:, :], oh2[:, :], ALU.add).then_inc(s_oh, 1)

            def positions(n):
                dve.wait_ge(s_pos, n + 1)
                dve.tensor_tensor(posb[:, :], rt_ps[:, 16:16 + E], count[:, :], ALU.add).then_inc(s_next, 1)

            def choose_rows(n):
                dve.wait_ge(s_next, 2 * n + 1)
                dve.tensor_tensor(count[:, :], rt_ps[:, 32:32 + E], count[:, :], ALU.add)
                dve.tensor_tensor_reduce(junk[0][:, :], oh1[:, :], posb[:, :], 1.0, 0.0, ALU.mult, ALU.add, slotf[:, 0:1])
                dve.tensor_tensor_reduce(junk[1][:, :], oh2[:, :], posb[:, :], 1.0, 0.0, ALU.mult, ALU.add,
                                         slotf[:, 1:2]).then_inc(s_next, 1)

            def keep_rows(n, u):
                dve.wait_ge(s_next, 2 * n + 2)
                dve.tensor_copy(slot[u][:, :], slotf[:, :]).then_inc(s_slot, 1)

            def attend(i, u):
                now, ahead = within(i, 0, T - 1), within(i, 0, T - 2)
                behind, router = within(i, 1, T), within(i, 2, T + 1)
                v = 1 - u
                if ahead:
                    diagonal(i + 1)
                if now:
                    p_lo(i, 0)
                if ahead:
                    masked(i + 1, v, 0)
                if now:
                    p_lo(i, 1)
                if behind:
                    row_sum(i - 1, v)
                if ahead:
                    masked(i + 1, v, 1)
                if behind:
                    row_reciprocal(i - 1)
                if router:
                    logits(i - 2)
                if ahead:
                    negated_max(i + 1, v)
                if behind:
                    add_attention(i - 1, v, 0)
                if router:
                    largest(i - 2)
                if behind:
                    add_attention(i - 1, v, 1)
                if now:
                    p_lo(i, 2)
                if behind:
                    stats1(i - 1)
                if router:
                    experts(i - 2)
                if behind:
                    moments1(i - 1)
                if router:
                    keep_top(i - 2)
                if within(i, 0, T - 3):
                    scores(i + 2, u)
                if router:
                    one_hots(i - 2)
                if behind:
                    normalise1(i - 1)
                if router:
                    both_hots(i - 2)
                if now:
                    p_lo(i, 3)
                if behind:
                    stats2(i - 1)
                if router:
                    positions(i - 2)
                if behind:
                    moments2(i - 1)
                if router:
                    choose_rows(i - 2)
                if behind:
                    normalise2(i - 1, v)
                if router:
                    keep_rows(i - 2, u)

            diagonal(0)
            scores(0, 0)
            scores(1, 1)
            masked(0, 0, 0)
            masked(0, 0, 1)
            negated_max(0, 0)
            steps(dve, attend)

            dve.wait_ge(s_slot, T)
            dve.tensor_copy(tail_row[0:1, :], count[0:1, :]).then_inc(s_tail_in, 1)
            link, n = chain(dve, s_ds, base)
            cnt, til, cum, one, nxt = (small[0:1, k * E:(k + 1) * E] for k in range(5))
            link(dve.scalar_tensor_tensor(out=cnt, in0=iota_e[0:1, :], scalar=-float(REGION), in1=count[0:1, :], op0=ALU.mult, op1=ALU.add))
            link(dve.tensor_scalar(nxt.bitcast(I32), cnt, R / 2 - 0.5, 1.0 / R, ALU.add, ALU.mult))
            link(dve.tensor_copy(til, nxt.bitcast(I32)))
            link(dve.memset(one, 1.0))
            link(dve.tensor_tensor_scan(cum, one, til, 0.0, ALU.mult, ALU.add))
            link(dve.tensor_scalar(nxt, til, -float(R), float(REGION), ALU.mult, ALU.add))
            ended, jump = (tb[:, k * E * FT:(k + 1) * E * FT].rearrange("o (e t) -> o e t", e=E) for k in range(2))
            t_of = iota_t[:, :].rearrange("o (a t) -> o a t", a=1).broadcast_to([1, E, FT])
            cum_of = cum.rearrange("o (e a) -> o e a", a=1).broadcast_to([1, E, FT])
            nxt_of = nxt.rearrange("o (e a) -> o e a", a=1).broadcast_to([1, E, FT])
            link(dve.tensor_tensor(ended, t_of, cum_of, ALU.is_ge))
            link(dve.tensor_tensor(jump, ended, nxt_of, ALU.mult))
            ex, row, past = (tb[:, (2 * E + k) * FT:(2 * E + k + 1) * FT] for k in range(3))
            link(dve.tensor_reduce(ex, ended[:, 0:E - 1, :].rearrange("o e t -> o t e"), mybir.AxisListType.X, ALU.add))
            link(dve.tensor_reduce(row, jump[:, 0:E - 1, :].rearrange("o e t -> o t e"), mybir.AxisListType.X, ALU.add))
            dve.tensor_copy(table_e[0:1, :], ex).then_inc(s_te, 1)
            link(dve.scalar_tensor_tensor(out=row, in0=iota_t[:, :], scalar=float(R), in1=row, op0=ALU.mult, op1=ALU.add))
            link(dve.tensor_scalar(past, row, -1.0, count[0:1, E - 1:E], ALU.mult, ALU.add))
            link(dve.tensor_tensor(past, past, ended[:, E - 1, :], ALU.mult))
            link(dve.tensor_tensor(row, row, past, ALU.add))
            dve.wait_ge(s_te, 1)
            dve.tensor_copy(table_row[0:1, :], row).then_inc(s_tab, 1)
            dve.wait_ge(s_top, T)
            dve.tensor_tensor(gate[:, 0, :], top_all[:, :, 1], top_all[:, :, 0], ALU.subtract).then_inc(s_d, 1)
            dve.wait_ge(s_ge, 1)
            link(dve.tensor_scalar(gate[:, 0, :], gate[:, 1, :], 1.0, None, ALU.add))
            link(dve.reciprocal(gate[:, 0, :], gate[:, 0, :]))
            link(dve.tensor_tensor(gate[:, 1, :], gate[:, 1, :], gate[:, 0, :], ALU.mult))
            for u in range(2):
                dve.wait_ge(s_sc[u], 32 * TO)

            def split_x(t):
                dve.wait_ge(s_xg, t + 1)
                if within(t, 1, FT):
                    dve.wait_ge(s_g1, 2 * t)
                dve.tensor_copy(x_hi[:, :], xg[:, :]).then_inc(s_xc, 1)
                dve.tensor_scalar(x_down[:, :], xg[:, :], 1.0 / LOSCALE, None, ALU.mult).then_inc(s_xc, 1)
                dve.wait_ge(s_xc, 2 * t + 2)
                dve.tensor_tensor(x_lo[:, :], xg[:, :], x_hi[:, :], ALU.subtract).then_inc(s_xh, 1)

            def split_h(t, u):
                dve.wait_ge(s_ge1, 2 * t + 2)
                if within(t, 2, FT):
                    dve.wait_ge(s_g2, t - 1)
                dve.tensor_copy(h_hi[u][:, :], hf[:, :]).then_inc(s_hc, 1)
                dve.wait_ge(s_hc, t + 1)
                dve.tensor_tensor(h_lo[u][:, :], hf[:, :], h_hi[u][:, :], ALU.subtract).then_inc(s_hh, 1)

            def result(t):
                e = dve.value_load(table_e[0:1, bass.ds(t, 1)], min_val=0, max_val=E - 1)
                dve.wait_ge(s_g2, t + 1)
                if within(t, 1, FT):
                    dve.wait_ge(s_ysc, 16 * S * t)
                for s in range(S):
                    dve.scalar_tensor_tensor(out=y_sb[:, s, :], in0=acc[s][:, D:2 * D], scalar=1.0 / LOSCALE,
                                             in1=b2_rep[:, bass.ds(e * D, D)], op0=ALU.mult, op1=ALU.add).then_inc(s_yc, 1)
                dve.wait_ge(s_yc, S * t + S)
                for s in range(S):
                    ins = dve.tensor_tensor(y_sb[:, s, :], acc[s][:, 0:D], y_sb[:, s, :], ALU.add)
                ins.then_inc(s_y, 1)

            split_x(0)
            split_x(1)
            split_h(0, 0)
            dve.wait_ge(s_b2, 16)

            def pair(t):
                split_x(t + 1)
                result(t - 1)
                split_h(t, 1)
                split_x(t + 2)
                result(t)
                split_h(t + 1, 0)

            pair(1)
            with dve.Fori(1, FT // 2 - 1) as o:
                pair(2 * o + 1)
            split_x(FT - 1)
            result(FT - 3)
            split_h(FT - 2, 1)
            result(FT - 2)
            split_h(FT - 1, 0)
            result(FT - 1)

            for c in range(YC):
                dve.wait_ge(s_yb[c], 16)
                for k in range(2):
                    for r in range(YT):
                        i = c * YT + r
                        if k == 1 and r == 0:
                            dve.wait_ge(s_cb, c + 1)
                        ins = dve.scalar_tensor_tensor(out=x_all[:, i, :], in0=y_all[:, i, k * D:(k + 1) * D],
                                                       scalar=gate[:, k, i:i + 1], in1=x_all[:, i, :],
                                                       op0=ALU.mult, op1=ALU.add)
                    ins.then_inc(s_cb if k == 0 else s_fin, 1)


_INS = ["x", "adj", "L0_gnn_W", "L0_gnn_a", "L0_ffn_Wr", "L0_ffn_br", "L0_ffn_ln_g", "L0_ffn_ln_b",
        "L0_ffn_W1", "L0_ffn_b1", "L0_ffn_W2", "L0_ffn_b2"]


def kernel(**inputs):
    import numpy as _np
    import concourse.bacc as _bacc
    from concourse import mybir as _mybir
    from concourse.bass_utils import run_bass_kernel_spmd as _run

    nc = _bacc.Bacc("TRN2", target_bir_lowering=False, num_devices=1)
    arrays, args = {}, []
    for name in _INS:
        a = _np.ascontiguousarray(inputs[name])
        arrays[f"in_{name}"] = a
        args.append(nc.dram_tensor(f"in_{name}", a.shape, _mybir.dt.from_np(a.dtype), kind="ExternalInput").ap())
    shape = inputs["x"].shape
    args.append(nc.dram_tensor("out_0", shape, _mybir.dt.float32, kind="ExternalOutput").ap())
    build(nc, *args)
    r = _run(nc, [arrays], core_ids=[0])
    return r.results[0]["out_0"]
```

```python
from contextlib import ExitStack

import concourse.bass as bass
from concourse import mybir

ALU = mybir.AluOpType
ACT = mybir.ActivationFunctionType
F32 = mybir.dt.float32
F16 = mybir.dt.float16
BF16 = mybir.dt.bfloat16
U32 = mybir.dt.uint32
I32 = mybir.dt.int32

P = 128
SLOPE = 0.2
LN_EPS = 1e-5
MASKED = 1.0e15
LOSCALE = 1024.0
PSCALE = 1024.0
DUMP = 256


def build(nc, x, adj, gnn_w, gnn_a, w_r, b_r, ln_g, ln_b, w1, b1, w2, b2, out):
    N, D = x.shape
    E = w_r.shape[1]
    HID = w1.shape[2]
    T = N // P
    KD = D // P
    HC = HID // P
    G = 4
    GJ = T // G
    GW = GJ * P
    HALF = N // 2
    S = 2
    R = S * P
    REGION = N + R
    ROW = D + 2
    CHUNKS = 4
    CW = KD * HID // 2
    GS = G - 1
    TS = GS * GJ
    XC = 8
    TC = T // XC
    FT = 2 * N // R + E - 1
    assert D == 256 and HID == 1024 and E == 8 and CW == 1024 and T % 4 == 0 and FT % 2 == 1 and R == DUMP

    rows_dram = nc.dram_tensor("rows_dram", [E * REGION, ROW], F32, kind="Internal").ap()
    wsplit_dram = nc.dram_tensor("wsplit_dram", [E * CHUNKS, P, 2 * CW], F16, kind="Internal").ap()

    adj_tiles = adj.rearrange("(t p) n -> t p n", p=P)
    x_view = x.rearrange("(t p) d -> p t d", p=P)
    out_view = out[0:N, :].rearrange("(t p) d -> p t d", p=P)
    w1_view = w1.rearrange("e (k p) h -> e k p h", p=P)
    w2_view = w2.rearrange("e (q c p) d -> e q p c d", q=2, p=P)

    with ExitStack() as ctx:
        def sb(name, shape, dt, stack=ctx):
            return stack.enter_context(nc.sbuf_tensor(name, shape, dt))

        def sem(name):
            return ctx.enter_context(nc.semaphore(name))

        def row_like(buffer, start, width):
            return buffer[:, start:start + width]

        tp = [ctx.enter_context(nc.psum_tensor(f"tp{u}", [P, GW], F32)) for u in range(2)]
        acc = [ctx.enter_context(nc.psum_tensor(f"acc{u}", [P, 2 * D], F32)) for u in range(2)]
        xt_ps = ctx.enter_context(nc.psum_tensor("xt_ps", [P, 512], F32))
        rt_ps = ctx.enter_context(nc.psum_tensor("rt_ps", [P, 512], F32))

        x_all = sb("x_all", [P, T, D], F32)
        ident = sb("ident", [P, P], F32)
        count = sb("count", [P, E], F32)
        table_e = sb("table_e", [1, FT], I32)
        table_row = sb("table_row", [1, FT], I32)
        tail_row = sb("tail_row", [1, E], I32)
        g_cols = sb("g_cols", [P, E, KD], F32)
        b_cols = sb("b_cols", [P, E, KD], F32)
        b1_cols = sb("b1_cols", [P, E, HC], F32)

        front = ExitStack()
        adj_sb = sb("adj_sb", [P, N], F32, front)
        bias_sb = sb("bias_sb", [P, N], BF16, front)
        t_row = sb("t_row", [P, N], F32, front)
        t2_row = sb("t2_row", [P, N], F32, front)
        sc = [sb(f"sc{u}", [P, N], F32, front) for u in range(2)]
        wh = sb("wh", [P, TS, 2, D], F16, front)
        wh32 = sb("wh32", [P, GJ, D], F32, front)
        pt_hi = [sb(f"pt_hi{g}", [P, GW], F16, front) for g in range(GS)]
        pt_lo = [sb(f"pt_lo{g}", [P, GW], F16, front) for g in range(GS)]
        pt32 = sb("pt32", [P, GW], F32, front)
        wf = [sb(f"wf{u}", [P, CW], F32, front) for u in range(2)]
        wsp = [sb(f"wsp{u}", [P, 2 * CW], F16, front) for u in range(2)]
        xn = [sb(f"xn{u}", [P, D], F32, front) for u in range(2)]
        xnt = [sb(f"xnt{u}", [P, D], F32, front) for u in range(2)]
        row_a = [sb(f"row_a{u}", [P, ROW], F32, front) for u in range(2)]
        row_b = [sb(f"row_b{u}", [P, ROW], F32, front) for u in range(2)]
        w_r_sb = sb("w_r_sb", [P, KD, E], F32, front)
        b_r_rep = sb("b_r_rep", [P, E], F32, front)
        s_col8 = sb("s_col8", [P, T], F32, front)
        half_neg = sb("half_neg", [P, T], F32, front)
        big = sb("big", [P, 1], F32, front)
        early = sb("early", [P, 1], F32, front)
        mx = sb("mx", [P, 2], F32, front)
        neg_m = [sb(f"neg_m{u}", [P, 1], F32, front) for u in range(2)]
        rsum = [sb(f"rsum{u}", [P, 2], F32, front) for u in range(2)]
        rinv = sb("rinv", [P, 2], F32, front)
        mv1 = sb("mv1", [P, 2], F32, front)
        mv2 = sb("mv2", [P, 2], F32, front)
        rs1 = sb("rs1", [P, 2], F32, front)
        rs2 = sb("rs2", [P, 2], F32, front)
        bs1 = sb("bs1", [P, 6], F32, front)
        bs2 = sb("bs2", [P, 6], F32, front)
        dest = sb("dest", [P, T], F32, front)
        gap_l = [sb(f"gap_l{u}", [P, 1], F32, front) for u in range(2)]
        exp_gap = [sb(f"exp_gap{u}", [P, 1], F32, front) for u in range(2)]
        both = sb("both", [P, 1], F32, front)
        tri = sb("tri", [P, P], BF16, front)
        ones = sb("ones", [P, P], BF16, front)
        off_diag = sb("off_diag", [P, P], BF16, front)
        iota_e = sb("iota_e", [P, E], F32, front)
        lg = sb("lg", [P, E], F32, front)
        top8 = sb("top8", [P, 8], F32, front)
        idx8 = sb("idx8", [P, 8], U32, front)
        idxf = sb("idxf", [P, 2], F32, front)
        oh1 = sb("oh1", [P, E], F32, front)
        oh2 = sb("oh2", [P, E], F32, front)
        oh = sb("oh", [P, E], BF16, front)
        posb = sb("posb", [P, E], F32, front)
        junk = [sb(f"junk{k}", [P, E], F32, front) for k in range(2)]
        slotf = sb("slotf", [P, 2], F32, front)
        slot = [sb(f"slot{u}", [P, 2], U32, front) for u in range(2)]
        wcat = row_like(sc[1], 0, KD * (D + 2)).rearrange("p (k n) -> p k n", k=KD)
        a_rep = row_like(sc[1], 1024, 2 * D).rearrange("p (k n) -> p k n", k=2)
        wa_rep = row_like(sc[1], 1536, KD * P).rearrange("p (k n) -> p k n", k=KD)
        bst = row_like(sc[1], 2048, T * 6).rearrange("p (t n) -> p t n", t=T)
        mean, var, rstd, s_col, gap = (row_like(sc[1], 2560 + T * k, T) for k in range(5))
        xn4 = [xn[0], xn[1], row_like(sc[1], 1792, D), row_like(sc[1], 2264, D)]
        wjunk = [row_like(sc[1], 3072 + k * 2 * D, 2 * D) for k in range(KD)]
        zrow = sb("zrow", [P, S * ROW], F32, front)
        tb = sb("tb", [1, 3 * E * FT], F32, front)
        iota_t = sb("iota_t", [1, FT], F32, front)
        small = sb("small", [P, 5 * E], F32, front)
        front.close()

        ffn_stack = ExitStack()
        w_sb = sb("w_sb", [P, E * CHUNKS * 2 * CW], F16, ffn_stack)
        w_blocks = w_sb[:, :].rearrange("p (b z n) -> p b z n", z=2, n=CW)
        b2_rep = sb("b2_rep", [P, E * D], F32, ffn_stack)
        xs = [sb(f"xs{u}", [P, S, ROW], F32, ffn_stack) for u in range(2)]
        xg = sb("xg", [P, KD * R], F32, ffn_stack)
        x_hi = sb("x_hi", [P, KD * R], F16, ffn_stack)
        x_lo = sb("x_lo", [P, KD * R], F16, ffn_stack)
        x_down = sb("x_down", [P, KD * R], F16, ffn_stack)
        hf = sb("hf", [P, HC * R], F32, ffn_stack)
        h_hi = [sb(f"h_hi{u}", [P, HC * R], F16, ffn_stack) for u in range(2)]
        h_lo = [sb(f"h_lo{u}", [P, HC * R], F16, ffn_stack) for u in range(2)]
        y_sb = sb("y_sb", [P, S, D], F32, ffn_stack)
        dump = sb("dump", [P, S], F32, ffn_stack)
        dz = sb("dz", [P, S], F32, ffn_stack)
        weight = [sb(f"weight{u}", [P, S], F32, ffn_stack) for u in range(2)]
        yidx = [sb(f"yidx{u}", [P, S], U32, ffn_stack) for u in range(2)]
        ffn_stack.close()

        s_top = sem("logit_gap_done")
        s_gt = sem("gate_step")
        s_te = sem("table_of_experts_done")
        s_wp = sem("w_chunk_rest_done")
        s_ve1 = sem("ln1_var_eps_done")
        s_ve2 = sem("ln2_var_eps_done")
        s_du = sem("dump_rows_done")
        s_dz = sem("dump_choice_done")
        s_x = [sem(f"x_loaded{c}") for c in range(XC)]
        s_par = sem("gnn_params_loaded")
        s_par2 = sem("ffn_params_loaded")
        s_pc = sem("pool_consts")
        s_ps = sem("pool_step")
        s_ds = sem("dve_step")
        s_apart = sem("carries_a_register_wait")
        s_st = sem("ln_stats_done")
        s_mom = sem("ln_moment_step")
        s_mean = sem("ln_mean_done")
        s_var = sem("ln_var_done")
        s_rstd = sem("rstd_done")
        s_xn = sem("xn_done")
        s_xnt_ps = sem("xnt_in_psum")
        s_xnt = sem("xnt_in_sbuf")
        s_wa = sem("wa_done")
        s_wh = sem("wh_in_psum")
        s_whh = sem("wh_hi_done")
        s_whl = sem("wh_lo_done")
        s_tr = sem("t_row_part_done")
        s_s8 = sem("s_cols_done")
        s_adj = [sem(f"adj_half_loaded{h}") for h in range(2)]
        s_mk = [sem(f"mask_half_done{h}") for h in range(2)]
        s_relu = sem("relu_branch_done")
        s_add = sem("pool_scores_done")
        s_c = sem("dve_scores_done")
        s_dg = sem("diagonal_unmasked")
        s_b = [sem(f"masked_half_done{h}") for h in range(2)]
        s_m = sem("neg_max_done")
        s_e = [sem(f"exp_half_done{h}") for h in range(2)]
        s_t = sem("p_transposed")
        s_hi = sem("p_hi_done")
        s_lo = sem("p_lo_done")
        s_av = sem("av_done")
        s_x1 = sem("x1_step")
        s_mv1 = sem("ln1_stats")
        s_r1 = sem("ln1_rstd")
        s_xl = sem("xl_done")
        s_xlp = sem("xl_t_in_psum")
        s_xlt = sem("xl_t_in_sbuf")
        s_mv2 = sem("ln2_stats")
        s_r2 = sem("ln2_rstd")
        s_row = sem("row_done")
        s_rows = sem("both_rows_done")
        s_lg = sem("logits_done")
        s_oh = sem("onehot_done")
        s_pos = sem("positions_done")
        s_slot = sem("slots_done")
        s_top2 = sem("router_step")
        s_next = sem("next_rows_step")
        s_st2 = sem("ln2_stats_first")
        s_sc = [sem(f"rows_scattered{u}") for u in range(2)]
        s_wf = [sem(f"w_chunk_loaded{u}") for u in range(2)]
        s_wc = [sem(f"w_chunk_hi_loaded{u}") for u in range(2)]
        s_wsp = sem("w_chunk_split")
        s_wst = [sem(f"w_chunk_stored{u}") for u in range(2)]
        s_tab = sem("table_done")
        s_tail_in = sem("tail_rows_done")
        s_tail = sem("tails_zeroed")
        s_ge = sem("gate_exp_done")
        s_wl = [sem(f"w_chunk_back{u}") for u in range(2)]
        s_wr = sem("w_ready_in_order")
        s_b2 = sem("b2_loaded")
        s_xs = [sem(f"xs_loaded{u}") for u in range(2)]
        s_xtp = sem("ffn_xt_in_psum")
        s_xg = sem("ffn_xt_scaled")
        s_xc = sem("ffn_x_hi_done")
        s_xh = sem("ffn_x_split")
        s_g1 = sem("ffn_hidden_half_in_psum")
        s_ge1 = sem("ffn_gelu_half_done")
        s_hc = sem("ffn_h_hi_done")
        s_hh = sem("ffn_hidden_split")
        s_g2 = sem("ffn_y_in_psum")
        s_yc = sem("ffn_y_low_added")
        s_y = sem("ffn_y_done")
        s_yi = sem("ffn_index_done")
        s_ysc = sem("y_scattered")
        s_out = sem("x1_stored")

        block = ctx.enter_context(nc.Block())

        def chain(eng, sem_, base):
            n = [0]

            def link(ins):
                n[0] += 1
                ins.then_inc(sem_, 1)
                eng.wait_ge(sem_, base + n[0])
            return link, n

        X1 = 4
        TOP = 5
        YI = 2 * S
        YA = 2 * S

        def apart(eng):
            eng.sem_inc(s_apart, 1)

        def within(i, first, last):
            return not isinstance(i, int) or first <= i <= last

        TO = T // 2

        def chunks(eng, chunk):
            chunk(0, 0, False)
            with eng.Fori(1, TS // TC) as c:
                chunk(c, c * TC, False)
            for c in range(TS // TC, XC + 1):
                chunk(c, c * TC, True)

        def steps(eng, body):
            for i in range(4):
                body(i, i % 2)
            with eng.Fori(2, TO - 1) as o:
                for u in range(2):
                    body(2 * o + u, u)
            for i in range(T - 2, T + 2):
                body(i, i % 2)

        @block.sync
        def _(sp):
            for c in range(XC):
                sp.dma_start(x_all[:, c * TC:(c + 1) * TC, :], x_view[:, c * TC:(c + 1) * TC, :]).then_inc(s_x[c], 16)
                if c == 0:
                    sp.dma_start(wcat[:, :, 0:D], gnn_w.rearrange("(k p) n -> p k n", p=P)).then_inc(s_par, 16)
                    sp.dma_start(a_rep[:, :, :],
                                 gnn_a.rearrange("(o k d) -> o k d", o=1, k=2).broadcast_to([P, 2, D])).then_inc(s_par, 16)

            def load_adj(i, h):
                sp.dma_start(adj_sb[:, h * HALF:(h + 1) * HALF], adj_tiles[i, :, h * HALF:(h + 1) * HALF]).then_inc(s_adj[h], 16)

            def load_w(e, q):
                src = w1_view[e, q] if q < 2 else w2_view[e, q - 2]
                dst = wf[q % 2][:, :]
                if q >= 2:
                    dst = dst.rearrange("p (c d) -> p c d", d=D)
                sp.dma_start(dst, src).then_inc(s_wf[q % 2], 16)

            def store_w(e, q):
                sp.wait_ge(s_wsp, CHUNKS * e + q + 1)
                sp.dma_start(wsplit_dram[CHUNKS * e + q], wsp[q % 2][:, :]).then_inc(s_wst[q % 2], 16)

            load_adj(0, 0)
            load_adj(0, 1)
            with nc.allow_non_contiguous_dma(reason="one column for each partition"):
                sp.dma_start(g_cols[:, :, :], ln_g.rearrange("e (k p) -> p e k", p=P)).then_inc(s_par2, 16)
                sp.dma_start(b_cols[:, :, :], ln_b.rearrange("e (k p) -> p e k", p=P)).then_inc(s_par2, 16)
                sp.dma_start(b1_cols[:, :, :], b1.rearrange("e (c p) -> p e c", p=P)).then_inc(s_par2, 16)
            sp.dma_start(w_r_sb[:, :, :], w_r.rearrange("(k p) e -> p k e", p=P)).then_inc(s_par2, 16)
            sp.dma_start(b_r_rep[:, :], b_r.rearrange("(o e) -> o e", o=1).broadcast_to([P, E])).then_inc(s_par2, 16)

            def store_x1(n):
                sp.wait_ge(s_x1, X1 * n + 3)
                sp.dma_start(out_view[:, bass.ds(n, 1), :], x_all[:, bass.ds(n, 1), :]).then_inc(s_out, 16)

            def tile_step(e, first=False, last=False):
                for q in range(CHUNKS):
                    i = CHUNKS * e + q
                    if not first:
                        store_x1(i - CHUNKS)
                    for h in range(2):
                        if not (last and q == CHUNKS - 1):
                            sp.wait_ge(s_mk[h], i + 1)
                            load_adj(i + 1, h)
                    if not (first and q < 2):
                        sp.wait_ge(s_wsp, i - 1)
                    load_w(e, q)
                    if q >= 1:
                        store_w(e, q - 1)
                    elif not first:
                        store_w(e - 1, CHUNKS - 1)

            sp.wait_ge(s_pc, 7)
            sp.dma_start(out[N:N + R, :].rearrange("(s p) d -> p s d", p=P),
                         zrow[:, 0:S * D].rearrange("p (s d) -> p s d", s=S)).then_inc(s_out, 16)
            tile_step(0, first=True)
            with sp.Fori(1, E - 1) as e:
                tile_step(e)
            tile_step(E - 1, last=True)
            store_w(E - 1, CHUNKS - 1)
            for u in range(2):
                sp.wait_ge(s_wst[u], 16 * E * CHUNKS // 2)

            def load_chunk(j):
                sp.dma_start(w_sb[:, j * 2 * CW:(j + 1) * 2 * CW], wsplit_dram[j]).then_inc(s_wl[j % 2], 16)

            for h in range(2):
                sp.wait_ge(s_mk[h], T)
            for q in range(CHUNKS):
                load_chunk(q)
            sp.wait_ge(s_tail_in, 1)
            for k in range(0, E, 2):
                row = sp.value_load(tail_row[0:1, k:k + 1], min_val=0, max_val=E * REGION - R)
                sp.dma_start(rows_dram[bass.ds(row, R), :].rearrange("(s p) d -> p s d", p=P),
                             zrow[:, :].rearrange("p (s d) -> p s d", s=S)).then_inc(s_tail, 16)
            sp.wait_ge(s_tail, 16 * E)
            for u in range(2):
                sp.wait_ge(s_sc[u], 32 * TO)
            sp.wait_ge(s_av, G * T)
            sp.wait_ge(s_slot, T)
            sp.wait_ge(s_tab, 1)
            for u in range(2):
                sp.wait_ge(s_xs[u], 16)
            for n in range(T - CHUNKS, T):
                store_x1(n)
            sp.wait_ge(s_m, T)
            sp.wait_ge(s_c, T)
            sp.wait_ge(s_relu, T)
            sp.wait_ge(s_add, 2 * T)
            sp.dma_start(b2_rep[:, :], b2.rearrange("(o e) d -> o (e d)", o=1).broadcast_to([P, E * D])).then_inc(s_b2, 16)
            for j in range(E * CHUNKS):
                sp.wait_ge(s_wl[j % 2], 16 * (j // 2 + 1))
                sp.sem_inc(s_wr, 1)
                if CHUNKS <= j + 2 < E * CHUNKS:
                    load_chunk(j + 2)

            sp.wait_ge(s_ysc, 16 * S * FT)

        @block.gpsimd
        def _(pool):
            pool.memset(ident[:, :], 0.0).then_inc(s_ps, 1)
            pool.memset(tri[:, :], 1.0).then_inc(s_ps, 1)
            pool.memset(half_neg[:, :], -0.5).then_inc(s_ps, 1)
            pool.memset(ones[:, :], 1.0).then_inc(s_ps, 1)
            pool.memset(zrow[:, :], 0.0).then_inc(s_ps, 1)
            pool.wait_ge(s_ps, 5)
            pool.affine_select(out=ident[:, :], in_=ident[:, :], compare_op=ALU.not_equal, fill=1.0, base=0,
                               pattern=[[-1, P]], channel_multiplier=1).then_inc(s_pc, 1)
            pool.affine_select(out=tri[:, :], in_=tri[:, :], compare_op=ALU.is_gt, fill=0.0, base=0,
                               pattern=[[1, P]], channel_multiplier=-1).then_inc(s_pc, 1)
            pool.affine_select(out=off_diag[:, :], in_=ones[:, :], compare_op=ALU.not_equal, fill=0.0, base=0,
                               pattern=[[-1, P]], channel_multiplier=1).then_inc(s_pc, 1)
            pool.iota(iota_e[:, :], [[1, E]], base=0, channel_multiplier=0,
                      allow_small_or_imprecise_dtypes=True).then_inc(s_pc, 1)
            pool.iota(count[:, :], [[REGION, E]], base=0, channel_multiplier=0,
                      allow_small_or_imprecise_dtypes=True).then_inc(s_pc, 1)
            pool.iota(iota_t[:, :], [[1, FT]], base=0, channel_multiplier=0,
                      allow_small_or_imprecise_dtypes=True).then_inc(s_pc, 1)
            pool.iota(dest[:, :], [[P, T]], base=1, channel_multiplier=1,
                      allow_small_or_imprecise_dtypes=True).then_inc(s_pc, 1)
            for c in range(XC):
                cols = slice(c * TC, (c + 1) * TC)
                pool.wait_ge(s_var, c + 1)
                pool.tensor_scalar(rstd[:, cols], var[:, cols], 1.0, LN_EPS, ALU.mult, ALU.add).then_inc(s_ps, 1)
                pool.wait_ge(s_ps, 6 + c)
                pool.tensor_tensor(rstd[:, cols], rstd[:, cols], half_neg[:, cols], ALU.pow).then_inc(s_rstd, 1)

            def scores(n, u, h):
                if h == 0:
                    pool.wait_ge(s_relu, n + 1)
                cols = slice(h * HALF // 2, (h + 1) * HALF // 2)
                pool.tensor_tensor(sc[u][:, cols], sc[u][:, cols], t2_row[:, cols], ALU.add).then_inc(s_add, 1)

            def cast_w(e, q):
                if not (isinstance(e, int) and e == 0 and q < 2):
                    pool.wait_ge(s_wst[q % 2], 16 * (2 * e + q // 2))
                    apart(pool)
                src = w1_view[e, q] if q < 2 else w2_view[e, q - 2]
                dst = wsp[q % 2][:, 0:CW]
                if q >= 2:
                    dst = dst.rearrange("p (c d) -> p c d", d=D)
                pool.dma_start(dst, src).then_inc(s_wc[q % 2], 16)

            def split_w(e, q):
                i = CHUNKS * e + q
                u = q % 2
                pool.wait_ge(s_wf[u], 16 * (2 * e + q // 2 + 1))
                pool.wait_ge(s_wc[u], 16 * (2 * e + q // 2 + 1))
                pool.tensor_tensor(wf[u][:, :], wf[u][:, :], wsp[u][:, 0:CW], ALU.subtract).then_inc(s_wp, 1)
                pool.wait_ge(s_wp, i + 1)
                apart(pool)
                pool.tensor_scalar(wsp[u][:, CW:2 * CW], wf[u][:, :], LOSCALE, 0.0, ALU.mult, ALU.add).then_inc(s_wsp, 1)

            def rstd1(n):
                pool.wait_ge(s_mv1, n + 1)
                apart(pool)
                pool.tensor_scalar(rs1[:, 0:1], mv1[:, 1:2], 1.0, LN_EPS, ALU.mult, ALU.add).then_inc(s_ve1, 1)
                pool.wait_ge(s_ve1, n + 1)
                pool.tensor_tensor(rs1[:, 1:2], rs1[:, 0:1], half_neg[:, 0:1], ALU.pow).then_inc(s_r1, 1)

            def rstd2(n):
                pool.wait_ge(s_mv2, n + 1)
                apart(pool)
                pool.tensor_scalar(rs2[:, 0:1], mv2[:, 1:2], 1.0, LN_EPS, ALU.mult, ALU.add).then_inc(s_ve2, 1)
                pool.wait_ge(s_ve2, n + 1)
                pool.tensor_tensor(rs2[:, 1:2], rs2[:, 0:1], half_neg[:, 0:1], ALU.pow).then_inc(s_r2, 1)

            def copy_row(n, u):
                pool.wait_ge(s_row, n + 1)
                apart(pool)
                pool.tensor_copy(row_b[u][:, 0:D], row_a[u][:, 0:D]).then_inc(s_rows, 1)
                pool.tensor_copy(row_a[u][:, D:D + 1], dest[:, bass.ds(n, 1)]).then_inc(s_rows, 1)
                pool.tensor_copy(row_b[u][:, D:D + 1], dest[:, bass.ds(n, 1)]).then_inc(s_rows, 1)

            def scatter_rows(n, u):
                pool.wait_ge(s_rows, 3 * n + 3)
                pool.wait_ge(s_slot, n + 1)
                pool.wait_ge(s_gt, 3 * n + 3)
                apart(pool)
                for k, rows in enumerate((row_a, row_b)):
                    pool.indirect_dma_start(
                        out=rows_dram[:, :], out_offset=bass.IndirectOffsetOnAxis(ap=slot[u][:, k:k + 1], axis=0),
                        in_=rows[u][:, :], in_offset=None).then_inc(s_sc[u], 16)

            def step(e, q):
                i = CHUNKS * e + q
                u = q % 2
                if within(i, 0, T - 2):
                    cast_w(e + (q + 1) // CHUNKS, (q + 1) % CHUNKS)
                if within(i, 0, T - 1):
                    split_w(e, q)
                if within(i, 2, T + 1):
                    copy_row(i - 2, u)
                if within(i, 3, T + 2):
                    scatter_rows(i - 3, 1 - u)
                if within(i, 0, T - 3):
                    scores(i + 2, u, 0)
                if within(i, 1, T):
                    rstd1(i - 1)
                if within(i, 0, T - 3):
                    scores(i + 2, u, 1)
                if within(i, 1, T):
                    rstd2(i - 1)

            cast_w(0, 0)
            for h in range(2):
                scores(0, 0, h)
            for h in range(2):
                scores(1, 1, h)
            for q in range(CHUNKS):
                step(0, q)
            with pool.Fori(1, E - 1) as e:
                for q in range(CHUNKS):
                    step(e, q)
            for i in range(T - CHUNKS, T + 3):
                step(i // CHUNKS, i % CHUNKS)

            for u in range(2):
                pool.wait_ge(s_sc[u], 32 * TO)
            pool.wait_ge(s_av, G * T)
            pool.wait_ge(s_tab, 1)
            pool.iota(dump[:, :], [[P, S]], base=N + 1, channel_multiplier=1,
                      allow_small_or_imprecise_dtypes=True).then_inc(s_du, 1)
            pool.wait_ge(s_du, 1)

            def index(o, u):
                t = 2 * o + u
                pool.wait_ge(s_xs[u], 16 * (o + 1))
                if within(t, 1, FT):
                    pool.wait_ge(s_yi, YI * t)
                apart(pool)
                for s in range(S):
                    pool.tensor_scalar(dz[:, s:s + 1], xs[u][:, s, D:D + 1], 0.0, dump[:, s:s + 1], ALU.is_equal,
                                       ALU.mult).then_inc(s_dz, 1)
                if within(t, 2, FT):
                    pool.wait_ge(s_ysc, 16 * S * (t - 1))
                pool.wait_ge(s_dz, S * t + S)
                apart(pool)
                for s in range(S):
                    pool.tensor_scalar(yidx[u][:, s:s + 1], xs[u][:, s, D:D + 1], -1.0, dz[:, s:s + 1], ALU.add, ALU.add).then_inc(s_yi, 1)
                for s in range(S):
                    pool.tensor_copy(weight[u][:, s:s + 1], xs[u][:, s, D + 1:D + 2]).then_inc(s_yi, 1)

            def scatter_y(t, u):
                pool.wait_ge(s_yi, YI * t + YI)
                pool.wait_ge(s_y, t + 1)
                apart(pool)
                for s in range(S):
                    pool.indirect_dma_start(
                        out=out[:, :], out_offset=bass.IndirectOffsetOnAxis(ap=yidx[u][:, s:s + 1], axis=0),
                        in_=y_sb[:, s, :], in_offset=None, compute_op=ALU.add).then_inc(s_ysc, 16)

            index(0, 0)
            index(0, 1)
            pool.wait_ge(s_out, 16 * (T + 1))
            scatter_y(0, 0)
            with pool.Fori(1, FT // 2) as o:
                index(o, 0)
                scatter_y(2 * o - 1, 1)
                index(o, 1)
                scatter_y(2 * o, 0)
            index(FT // 2, 0)
            scatter_y(FT - 2, 1)
            scatter_y(FT - 1, 0)

        @block.tensor
        def _(pe):
            pe.wait_ge(s_pc, 7)

            def project_t(i, k4):
                u = k4 % 2
                pe.wait_ge(s_xn, i + 1)
                if within(i, 2, T):
                    pe.wait_ge(s_xnt, i - 1)
                for k in range(KD):
                    m = pe.transpose(tp[u][:, k * P:(k + 1) * P], xn4[k4][:, k * P:(k + 1) * P], ident[:, :])
                m.then_inc(s_xnt_ps, 1)

            def project(i, u):
                pe.wait_ge(s_xnt, i + 1)
                if within(i, 2, T):
                    pe.wait_ge(s_whl, i - 1)
                    pe.wait_ge(s_tr, 2 * i - 2)
                for k in range(KD):
                    pe.matmul(tp[u][:, 512:512 + D + 2], xnt[u][:, k * P:(k + 1) * P], wcat[:, k, :],
                              start=(k == 0), stop=(k == KD - 1))
                for k in range(KD):
                    m = pe.matmul(acc[u][:, 0:P], wa_rep[:, k, :], xnt[u][:, k * P:(k + 1) * P],
                                  start=(k == 0), stop=(k == KD - 1))
                m.then_inc(s_wh, 1)

            def first_steps(c, start, late):
                for k in range(min(TC, T + 2 - start) if isinstance(start, int) else TC):
                    first_step(start + k, k)

            def first_step(i, k):
                u = k % 2
                if within(i, 0, T - 1):
                    project_t(i, k)
                if isinstance(i, int) and i == 1:
                    pe.wait_ge(s_wa, 1)
                if within(i, 1, T):
                    project(i - 1, 1 - u)

            chunks(pe, first_steps)

            def p_transpose(i, u, g):
                if g % 2 == 0:
                    pe.wait_ge(s_e[g // 2], i + 1)
                if g == 1:
                    if within(i, 1, T):
                        pe.wait_ge(s_hi, G * i)
                elif g > 1 or within(i, 1, T):
                    pe.wait_ge(s_lo, GS * i + max(g - 1, 0))
                for c in range(GJ):
                    m = pe.transpose(tp[g % 2][:, c * P:(c + 1) * P], sc[u][:, (GJ * g + c) * P:(GJ * g + c + 1) * P], ident[:, :])
                m.then_inc(s_t, 1)

            def av(i, u, g):
                o = acc[u][:, 0:D]
                if g < GS:
                    pe.wait_ge(s_lo, GS * i + g + 1)
                else:
                    pe.wait_ge(s_hi, G * i + G)
                if g == 0 and within(i, 2, T):
                    pe.wait_ge(s_x1, X1 * (i - 2) + 3)
                for c in range(GJ):
                    j = GJ * g + c
                    cols = slice(c * P, (c + 1) * P)
                    if g < GS:
                        pe.matmul(o, pt_hi[g][:, cols], wh[:, j, 0, :], start=(j == 0), stop=False)
                        pe.matmul(o, pt_hi[g][:, cols], wh[:, j, 1, :], start=False, stop=False)
                        m = pe.matmul(o, pt_lo[g][:, cols], wh[:, j, 0, :], start=False, stop=False)
                    else:
                        m = pe.matmul(o, pt32[:, cols], wh32[:, c, :], start=False, stop=(c == GJ - 1))
                m.then_inc(s_av, 1)

            def router_t(i):
                pe.wait_ge(s_xl, i + 1)
                for k in range(KD):
                    m = pe.transpose(xt_ps[:, k * P:(k + 1) * P], xn[0][:, k * P:(k + 1) * P], ident[:, :])
                m.then_inc(s_xlp, 1)

            def router_mm(i):
                pe.wait_ge(s_xlt, i + 1)
                if within(i, 1, T):
                    pe.wait_ge(s_slot, i)
                for k in range(KD):
                    m = pe.matmul(rt_ps[:, 0:E], xnt[0][:, k * P:(k + 1) * P], w_r_sb[:, k, :], start=(k == 0), stop=(k == KD - 1))
                m.then_inc(s_lg, 1)

            def router_pos(i):
                pe.wait_ge(s_oh, i + 1)
                pe.matmul(rt_ps[:, 16:16 + E], tri[:, :], oh[:, :], start=True, stop=True)
                pe.matmul(rt_ps[:, 32:32 + E], ones[:, :], oh[:, :], start=True, stop=True).then_inc(s_pos, 1)

            def attend(i, u):
                now = within(i, 0, T - 1)
                if now:
                    p_transpose(i, u, 0)
                    p_transpose(i, u, 1)
                if within(i, 1, T):
                    av(i - 1, 1 - u, 3)
                if within(i, 2, T + 1):
                    router_t(i - 2)
                if now:
                    av(i, u, 0)
                if within(i, 2, T + 1):
                    router_mm(i - 2)
                if now:
                    p_transpose(i, u, 2)
                    av(i, u, 1)
                    p_transpose(i, u, 3)
                    av(i, u, 2)
                if within(i, 2, T + 1):
                    router_pos(i - 2)

            pe.wait_ge(s_whl, T)
            steps(pe, attend)

            def ffn_t(o, u):
                pe.wait_ge(s_xs[u], 16 * (o + 1))
                if within(2 * o + u, 1, FT):
                    pe.wait_ge(s_xg, 2 * o + u)
                for k in range(KD):
                    for s in range(S):
                        m = pe.transpose(xt_ps[:, k * R + s * P:k * R + (s + 1) * P], xs[u][:, s, k * P:(k + 1) * P], ident[:, :])
                m.then_inc(s_xtp, 1)

            def expert_of(t):
                return pe.value_load(table_e[0:1, bass.ds(t, 1)], min_val=0, max_val=E - 1)

            def up(t):
                e = expert_of(t)
                pe.wait_ge(s_wr, e * CHUNKS + CHUNKS)
                pe.wait_ge(s_xh, t + 1)
                for c in range(HC):
                    if c % (HC // 2) == 0 and within(t, 1, FT):
                        pe.wait_ge(s_ge1, 2 * t - 1 + c // (HC // 2))
                    o = tp[c // 4][:, (c % 4) * R:(c % 4 + 1) * R]
                    for k in range(KD):
                        at = e * (CHUNKS * 2 * CW) + k * 2 * CW + c * P
                        w_hi = w_sb[:, bass.ds(at, P)]
                        w_lo = w_sb[:, bass.ds(at + CW, P)]
                        cols = slice(k * R, (k + 1) * R)
                        pe.matmul(o, w_hi, x_hi[:, cols], start=(k == 0), stop=False)
                        pe.matmul(o, w_hi, x_lo[:, cols], start=False, stop=False)
                        m = pe.matmul(o, w_lo, x_down[:, cols], start=False, stop=(k == KD - 1))
                    if c % (HC // 2) == HC // 2 - 1:
                        m.then_inc(s_g1, 1)

            def down(t, u):
                e = expert_of(t)
                pe.wait_ge(s_hh, t + 1)
                if within(t, 1, FT):
                    pe.wait_ge(s_yc, YA * t)
                for c in range(HC):
                    w_both = w_blocks[:, bass.ds(e * CHUNKS + 2 + c // 4, 1), :, (c % 4) * D:(c % 4 + 1) * D].rearrange("p a z n -> p (a z) n")
                    w_hi = w_both[:, 0, :]
                    for s in range(S):
                        pe.matmul(acc[s][:, :], h_hi[u][:, c * R + s * P:c * R + (s + 1) * P], w_both,
                                  start=(c == 0), stop=False, skip_group_check=True)
                    for s in range(S):
                        m = pe.matmul(acc[s][:, 0:D], h_lo[u][:, c * R + s * P:c * R + (s + 1) * P], w_hi,
                                      start=False, stop=(c == HC - 1), skip_group_check=True)
                m.then_inc(s_g2, 1)

            pe.wait_ge(s_tab, 1)
            for u in range(2):
                pe.wait_ge(s_sc[u], 32 * TO)
            ffn_t(0, 0)
            ffn_t(0, 1)
            up(0)

            def pair(o):
                up(2 * o + 1)
                ffn_t(o + 1, 0)
                down(2 * o, 0)
                up(2 * o + 2)
                ffn_t(o + 1, 1)
                down(2 * o + 1, 1)

            pair(0)
            with pe.Fori(1, FT // 2 - 1) as o:
                pair(o)
            up(FT - 2)
            ffn_t(FT // 2, 0)
            down(FT - 3, 0)
            up(FT - 1)
            down(FT - 2, 1)
            down(FT - 1, 0)

        @block.scalar
        def _(act):
            def mask(n, h):
                act.wait_ge(s_adj[h], 16 * (n + 1))
                if within(n, 1, T):
                    act.wait_ge(s_b[h], n)
                cols = slice(h * HALF, (h + 1) * HALF)
                act.activation(bias_sb[:, cols], adj_sb[:, cols], ACT.Relu, bias=big[:, 0:1], scale=-3.0e38).then_inc(s_mk[h], 1)

            def first_steps(c, start, late):
                if isinstance(c, int) and TS // TC <= c < XC:
                    mask(0, c - TS // TC)
                for k in range(min(TC, T + 2 - start) if isinstance(start, int) else TC):
                    first_step(start + k, k % 2, late)

            def first_step(i, u, late):
                if within(i, 0, T - 1):
                    act.wait_ge(s_xnt_ps, i + 1)
                    if within(i, 2, T):
                        act.wait_ge(s_wh, i - 1)
                    act.activation(xnt[u][:, :], tp[u][:, 0:D], ACT.Copy).then_inc(s_xnt, 1)
                if within(i, 1, T):
                    n, v = i - 1, 1 - u
                    late = n >= TS if isinstance(n, int) else late
                    act.wait_ge(s_wh, n + 1)
                    dst = wh32[:, bass.ds(n - TS, 1), :] if late else wh[:, bass.ds(n, 1), 0, :]
                    act.activation(dst, tp[v][:, 512:512 + D], ACT.Copy).then_inc(s_whh, 1)
                    act.activation(t_row[:, bass.ds(n * P, P)], acc[v][:, 0:P], ACT.Copy).then_inc(s_tr, 1)
                    act.activation(t2_row[:, bass.ds(n * P, P)], acc[v][:, 0:P], ACT.Copy, scale=SLOPE).then_inc(s_tr, 1)

            act.wait_ge(s_ds, 1)
            act.activation(early[:, :], big[:, :], ACT.Copy)
            chunks(act, first_steps)

            def relu_branch(n, u):
                if within(n, 2, T):
                    act.wait_ge(s_t, G * (n - 2) + 2)
                act.activation(sc[u][:, 0:HALF], t_row[:, 0:HALF], ACT.Relu, bias=s_col8[:, bass.ds(n, 1)],
                               scale=1.0 - SLOPE).then_inc(s_relu, 1)

            def exps(n, u, h):
                if h == 0:
                    act.wait_ge(s_m, n + 1)
                cols = slice(h * HALF, (h + 1) * HALF)
                act.activation(sc[u][:, cols], sc[u][:, cols], ACT.Exp, bias=neg_m[u][:, 0:1], scale=1.0,
                               accum_out=rsum[u][:, h:h + 1]).then_inc(s_e[h], 1)

            def p_hi(i, g):
                act.wait_ge(s_t, G * i + g + 1)
                if within(i, 1, T):
                    act.wait_ge(s_av, G * i + g - 3)
                dst = pt_hi[g] if g < GS else pt32
                act.activation(dst[:, :], tp[g % 2][:, :], ACT.Copy, scale=PSCALE).then_inc(s_hi, 1)

            def gate_exp(n, u):
                act.wait_ge(s_top, n + 1)
                act.activation(exp_gap[u][:, :], gap_l[u][:, :], ACT.Exp).then_inc(s_ge, 1)

            def router(n):
                act.wait_ge(s_xlp, n + 1)
                act.activation(xnt[0][:, :], xt_ps[:, 0:D], ACT.Copy).then_inc(s_xlt, 1)

            def attend(i, u):
                now = within(i, 0, T - 1)
                ahead = within(i, 0, T - 3)
                if now:
                    p_hi(i, 0)
                    p_hi(i, 1)
                    exps(i, u, 1)
                if within(i, 2, T + 1):
                    router(i - 2)
                if ahead:
                    relu_branch(i + 2, u)
                if now:
                    p_hi(i, 2)
                if ahead:
                    mask(i + 2, 0)
                if within(i, 0, T - 2):
                    exps(i + 1, 1 - u, 0)
                if now:
                    p_hi(i, 3)
                if within(i, 2, T + 1):
                    gate_exp(i - 2, u)
                if ahead:
                    mask(i + 2, 1)

            act.wait_ge(s_s8, 2)
            act.wait_ge(s_tr, 2 * T)
            relu_branch(0, 0)
            relu_branch(1, 1)
            mask(1, 0)
            exps(0, 0, 0)
            mask(1, 1)
            steps(act, attend)
            act.wait_ge(s_tail_in, 1)
            for k in range(1, E, 2):
                row = act.value_load(tail_row[0:1, k:k + 1], min_val=0, max_val=E * REGION - R)
                act.dma_start(rows_dram[bass.ds(row, R), :].rearrange("(s p) d -> p s d", p=P),
                              zrow[:, :].rearrange("p (s d) -> p s d", s=S)).then_inc(s_tail, 16)

            def load_x(o, u):
                if within(o, 1, FT):
                    act.wait_ge(s_yi, YI * (2 * o + u - 1))
                row = act.value_load(table_row[0:1, bass.ds(2 * o + u, 1)], min_val=0, max_val=E * REGION - R)
                act.dma_start(xs[u][:, :, :], rows_dram[bass.ds(row, R), :].rearrange("(s p) d -> p s d", p=P)).then_inc(s_xs[u], 16)

            def expert_of(t):
                return act.value_load(table_e[0:1, bass.ds(t, 1)], min_val=0, max_val=E - 1)

            def scaled(t):
                e = expert_of(t)
                act.wait_ge(s_xtp, t + 1)
                if within(t, 1, FT):
                    act.wait_ge(s_xh, t)
                for k in range(KD):
                    ins = act.activation(xg[:, k * R:(k + 1) * R], xt_ps[:, k * R:(k + 1) * R], ACT.Identity,
                                         bias=b_cols[:, bass.ds(e, 1), k], scale=g_cols[:, bass.ds(e, 1), k])
                ins.then_inc(s_xg, 1)

            def gelu(t):
                e = expert_of(t)
                for c in range(HC):
                    if c % (HC // 2) == 0:
                        act.wait_ge(s_g1, 2 * t + 1 + c // (HC // 2))
                        if c == 0 and within(t, 1, FT):
                            act.wait_ge(s_hh, t)
                    ins = act.activation(hf[:, c * R:(c + 1) * R], tp[c // 4][:, (c % 4) * R:(c % 4 + 1) * R], ACT.Gelu,
                                         bias=b1_cols[:, bass.ds(e, 1), c])
                    if c % (HC // 2) == HC // 2 - 1:
                        ins.then_inc(s_ge1, 1)

            act.wait_ge(s_tab, 1)
            for u in range(2):
                act.wait_ge(s_sc[u], 32 * TO)
            act.wait_ge(s_tail, 16 * E)
            act.wait_ge(s_av, G * T)
            load_x(0, 0)
            load_x(0, 1)
            scaled(0)

            def pair(o, first=False, last=False):
                scaled(2 * o + 1)
                if first:
                    load_x(o + 1, 0)
                gelu(2 * o)
                if not first:
                    load_x(o + 1, 0)
                scaled(2 * o + 2)
                gelu(2 * o + 1)
                if not last:
                    load_x(o + 1, 1)

            pair(0, first=True)
            with act.Fori(1, FT // 2 - 1) as o:
                pair(o)
            pair(FT // 2 - 1, last=True)
            gelu(FT - 1)

        @block.vector
        def _(dve):
            def tile_of(i):
                return x_all[:, bass.ds(i, 1), :].rearrange("p a d -> p (a d)")

            link, n = chain(dve, s_ds, 0)
            link(dve.memset(big[:, :], MASKED))

            def project_a():
                dve.wait_ge(s_par, 16 * 2)
                dve.wait_ge(s_pc, 7)
                for k in range(KD):
                    for h in range(2):
                        ins = dve.tensor_tensor_reduce(wjunk[k][:, h * D:(h + 1) * D], wcat[:, k, 0:D], a_rep[:, h, :], 1.0, 0.0,
                                                       ALU.mult, ALU.add, wcat[:, k, D + h:D + h + 1])
                link(ins)
                for k in range(KD):
                    ins = dve.tensor_scalar(wa_rep[:, k, :], ones[:, :], wcat[:, k, D + 1:D + 2], None, ALU.mult)
                ins.then_inc(s_wa, 1)

            def stats(i):
                dve.bn_stats(bst[:, bass.ds(i, 1), :].rearrange("p a d -> p (a d)"), tile_of(i)).then_inc(s_st, 1)

            def moments(c):
                m, v, g = (buffer[:, bass.ds(c * TC, TC)] for buffer in (mean, var, gap))
                b = bst[:, bass.ds(c * TC, TC), :]
                dve.wait_ge(s_st, TC * c + TC)
                dve.tensor_tensor(m, b[:, :, 1], b[:, :, 4], ALU.add)
                dve.tensor_tensor(g, b[:, :, 1], b[:, :, 4], ALU.subtract)
                dve.tensor_tensor(v, b[:, :, 2], b[:, :, 5], ALU.add).then_inc(s_mom, 1)
                dve.wait_ge(s_mom, 3 * c + 1)
                dve.scalar_tensor_tensor(out=g, in0=g, scalar=D / 4.0, in1=g, op0=ALU.mult, op1=ALU.mult).then_inc(s_mom, 1)
                dve.wait_ge(s_mom, 3 * c + 2)
                dve.tensor_tensor(v, v, g, ALU.add).then_inc(s_mom, 1)
                dve.wait_ge(s_mom, 3 * c + 3)
                dve.tensor_scalar(v, v, 1.0 / D, None, ALU.mult).then_inc(s_var, 1)
                dve.tensor_scalar(m, m, 0.5, None, ALU.mult).then_inc(s_mean, 1)

            def normalise(i, k):
                if within(i, TC, T):
                    dve.wait_ge(s_xnt_ps, i - TC + 1)
                dve.tensor_scalar(xn4[k][:, :], tile_of(i), mean[:, bass.ds(i, 1)], rstd[:, bass.ds(i, 1)],
                                  ALU.subtract, ALU.mult).then_inc(s_xn, 1)

            def first_steps(c, start, late):
                static = isinstance(c, int)
                more = not static or c + 1 < XC
                for k in range(min(TC, T + 2 - start) if static else TC):
                    if k == 0 and more:
                        moments(c + 1)
                    if k == 2 and more:
                        dve.wait_ge(s_rstd, c + 2)
                        dve.wait_ge(s_mean, c + 2)
                    first_step(start + k, k, late)
                    if not late:
                        stats(start + k + 2 * TC)
                if static and c == 0:
                    for d in range(3, XC):
                        dve.wait_ge(s_x[d], 16)

            def first_step(i, k, late):
                if within(i, 0, T - 3):
                    normalise(i + 2, (k + 2) % TC)
                if within(i, 2, T + 1):
                    n, u = i - 2, k % 2
                    late = n >= TS if isinstance(n, int) else late
                    dve.wait_ge(s_whh, n + 1)
                    ins = dve.tensor_copy(s_col[:, bass.ds(n, 1)], tp[u][:, 512 + D:512 + D + 1])
                    if not late:
                        ins = dve.tensor_tensor(wh[:, bass.ds(n, 1), 1, :], tp[u][:, 512:512 + D], wh[:, bass.ds(n, 1), 0, :],
                                                ALU.subtract)
                    ins.then_inc(s_whl, 1)

            for c in range(2):
                dve.wait_ge(s_x[c], 16)
                for i in range(TC):
                    stats(c * TC + i)
                if c == 0:
                    moments(c)
                    project_a()
            dve.wait_ge(s_x[2], 16)
            dve.wait_ge(s_rstd, 1)
            dve.wait_ge(s_mean, 1)
            for i in range(2):
                normalise(i, i)
            chunks(dve, first_steps)
            base = n[0]
            dve.wait_ge(s_whl, T)
            dve.tensor_scalar(s_col8[:, :], s_col, 1.0 - SLOPE, None, ALU.mult).then_inc(s_s8, 1)
            dve.wait_ge(s_s8, 1)
            dve.wait_ge(s_wh, T)
            dve.wait_ge(s_par2, 16 * 5)
            dve.sem_inc(s_s8, 1)
            dve.wait_ge(s_tr, 2 * T)

            def scores(n, u):
                if within(n, 2, T):
                    dve.wait_ge(s_t, G * (n - 1))
                dve.scalar_tensor_tensor(out=sc[u][:, HALF:N], in0=t_row[:, HALF:N], scalar=s_col8[:, bass.ds(n, 1)],
                                         in1=t2_row[:, HALF:N], op0=ALU.add, op1=ALU.max).then_inc(s_c, 1)

            def diagonal(n):
                for k in range(2):
                    dve.wait_ge(s_mk[k], n + 1)
                diag = bias_sb[:, bass.ds(n * P, P)]
                dve.tensor_tensor(diag, diag, off_diag[:, :], ALU.mult).then_inc(s_dg, 1)

            def masked(n, u, h):
                if h == 0:
                    dve.wait_ge(s_add, 2 * n + 2)
                else:
                    dve.wait_ge(s_c, n + 1)
                dve.wait_ge(s_dg, n + 1)
                apart(dve)
                cols = slice(h * HALF, (h + 1) * HALF)
                dve.tensor_tensor_reduce(sc[u][:, cols], sc[u][:, cols], bias_sb[:, cols], 1.0, -3.0e38,
                                         ALU.subtract, ALU.max, mx[:, h:h + 1]).then_inc(s_b[h], 1)

            def negated_max(n, u):
                for k in range(2):
                    dve.wait_ge(s_b[k], n + 1)
                dve.tensor_scalar(neg_m[u][:, :], mx[:, 0:1], mx[:, 1:2], -1.0, ALU.max, ALU.mult).then_inc(s_m, 1)

            def p_lo(i, g):
                dve.wait_ge(s_hi, G * i + g + 1)
                dve.scalar_tensor_tensor(out=pt_lo[g][:, :], in0=tp[g % 2][:, :], scalar=PSCALE, in1=pt_hi[g][:, :],
                                         op0=ALU.mult, op1=ALU.subtract).then_inc(s_lo, 1)

            def row_sum(n, u):
                dve.wait_ge(s_av, G * n + G)
                dve.wait_ge(s_e[1], n + 1)
                dve.tensor_scalar(rinv[:, 0:1], rsum[u][:, 0:1], rsum[u][:, 1:2], PSCALE, ALU.add, ALU.mult).then_inc(s_x1, 1)

            def row_reciprocal(n):
                dve.wait_ge(s_x1, X1 * n + 1)
                dve.reciprocal(rinv[:, 1:2], rinv[:, 0:1]).then_inc(s_x1, 1)

            def add_attention(n, u):
                dve.wait_ge(s_x1, X1 * n + 2)
                dve.scalar_tensor_tensor(out=tile_of(n), in0=acc[u][:, 0:D], scalar=rinv[:, 1:2], in1=tile_of(n),
                                         op0=ALU.mult, op1=ALU.add).then_inc(s_x1, 1)

            def stats1(n):
                dve.wait_ge(s_x1, X1 * n + 3)
                apart(dve)
                dve.bn_stats(bs1[:, :], tile_of(n)).then_inc(s_x1, 1)

            def moments1(n):
                dve.wait_ge(s_x1, X1 * n + 4)
                if within(n, 1, T):
                    dve.wait_ge(s_r1, n)
                apart(dve)
                dve.bn_aggr(mv1[:, :], bs1[:, :]).then_inc(s_mv1, 1)

            def normalise1(n):
                dve.wait_ge(s_r1, n + 1)
                dve.wait_ge(s_mv1, n + 1)
                if within(n, 1, T):
                    dve.wait_ge(s_xlp, n)
                dve.tensor_scalar(xn[0][:, :], tile_of(n), mv1[:, 0:1], rs1[:, 1:2], ALU.subtract, ALU.mult).then_inc(s_xl, 1)

            def stats2(n):
                dve.wait_ge(s_xl, n + 1)
                apart(dve)
                dve.bn_stats(bs2[:, :], xn[0][:, :]).then_inc(s_st2, 1)

            def moments2(n):
                dve.wait_ge(s_st2, n + 1)
                if within(n, 1, T):
                    dve.wait_ge(s_r2, n)
                apart(dve)
                dve.bn_aggr(mv2[:, :], bs2[:, :]).then_inc(s_mv2, 1)

            def normalise2(n, u):
                dve.wait_ge(s_r2, n + 1)
                dve.wait_ge(s_mv2, n + 1)
                if within(n, 2, T):
                    dve.wait_ge(s_sc[u], 16 * (n - u))
                dve.tensor_scalar(row_a[u][:, 0:D], xn[0][:, :], mv2[:, 0:1], rs2[:, 1:2], ALU.subtract,
                                  ALU.mult).then_inc(s_row, 1)

            def logits(n):
                dve.wait_ge(s_lg, n + 1)
                dve.tensor_tensor(lg[:, :], rt_ps[:, 0:E], b_r_rep[:, :], ALU.add).then_inc(s_top2, 1)

            def largest(n):
                dve.wait_ge(s_top2, TOP * n + 1)
                apart(dve)
                dve.max(top8[:, :], lg[:, :]).then_inc(s_top2, 1)

            def experts(n):
                dve.wait_ge(s_top2, TOP * n + 2)
                apart(dve)
                dve.max_index(idx8[:, :], top8[:, :], lg[:, :]).then_inc(s_top2, 1)

            def keep_top(n, u):
                dve.tensor_tensor(gap_l[u][:, :], top8[:, 1:2], top8[:, 0:1], ALU.subtract).then_inc(s_top, 1)
                dve.wait_ge(s_top2, TOP * n + 3)
                dve.tensor_copy(idxf[:, :], idx8[:, 0:2]).then_inc(s_top2, 1)

            def one_hots(n):
                dve.wait_ge(s_top2, TOP * n + 4)
                dve.tensor_scalar(oh1[:, :], iota_e[:, :], idxf[:, 0:1], None, ALU.is_equal)
                dve.tensor_scalar(oh2[:, :], iota_e[:, :], idxf[:, 1:2], None, ALU.is_equal).then_inc(s_top2, 1)

            def both_hots(n):
                dve.wait_ge(s_top2, TOP * n + 5)
                dve.tensor_tensor(oh[:, :], oh1[:, :], oh2[:, :], ALU.add).then_inc(s_oh, 1)

            def positions(n):
                dve.wait_ge(s_pos, n + 1)
                dve.tensor_tensor(posb[:, :], rt_ps[:, 16:16 + E], count[:, :], ALU.add).then_inc(s_next, 1)

            def choose_rows(n):
                dve.wait_ge(s_next, 2 * n + 1)
                dve.tensor_tensor(count[:, :], rt_ps[:, 32:32 + E], count[:, :], ALU.add)
                dve.tensor_tensor_reduce(junk[0][:, :], oh1[:, :], posb[:, :], 1.0, 0.0, ALU.mult, ALU.add, slotf[:, 0:1])
                dve.tensor_tensor_reduce(junk[1][:, :], oh2[:, :], posb[:, :], 1.0, 0.0, ALU.mult, ALU.add,
                                         slotf[:, 1:2]).then_inc(s_next, 1)

            def keep_rows(n, u):
                dve.wait_ge(s_next, 2 * n + 2)
                dve.tensor_copy(slot[u][:, :], slotf[:, :]).then_inc(s_slot, 1)

            def gate_sum(n, u):
                dve.wait_ge(s_ge, n + 1)
                dve.tensor_scalar(both[:, :], exp_gap[u][:, :], 1.0, None, ALU.add).then_inc(s_gt, 1)

            def gate_first(n, u):
                dve.wait_ge(s_gt, 3 * n + 1)
                dve.reciprocal(row_a[u][:, D + 1:D + 2], both[:, :]).then_inc(s_gt, 1)

            def gate_second(n, u):
                dve.wait_ge(s_gt, 3 * n + 2)
                dve.tensor_tensor(row_b[u][:, D + 1:D + 2], exp_gap[u][:, :], row_a[u][:, D + 1:D + 2], ALU.mult).then_inc(s_gt, 1)

            def attend(i, u):
                now, ahead = within(i, 0, T - 1), within(i, 0, T - 2)
                behind, router = within(i, 1, T), within(i, 2, T + 1)
                v = 1 - u
                gates = within(i, 3, T + 1)
                if gates:
                    gate_sum(i - 3, v)
                if ahead:
                    diagonal(i + 1)
                if now:
                    p_lo(i, 0)
                if gates:
                    gate_first(i - 3, v)
                if router:
                    normalise2(i - 2, u)
                if now:
                    p_lo(i, 1)
                if gates:
                    gate_second(i - 3, v)
                if ahead:
                    masked(i + 1, v, 0)
                if behind:
                    row_sum(i - 1, v)
                if ahead:
                    masked(i + 1, v, 1)
                if behind:
                    row_reciprocal(i - 1)
                if router:
                    logits(i - 2)
                if ahead:
                    negated_max(i + 1, v)
                if behind:
                    add_attention(i - 1, v)
                if router:
                    largest(i - 2)
                if behind:
                    stats1(i - 1)
                if router:
                    experts(i - 2)
                if now:
                    p_lo(i, 2)
                if behind:
                    moments1(i - 1)
                if router:
                    keep_top(i - 2, u)
                    one_hots(i - 2)
                    both_hots(i - 2)
                if within(i, 0, T - 3):
                    scores(i + 2, u)
                if behind:
                    normalise1(i - 1)
                    stats2(i - 1)
                if router:
                    positions(i - 2)
                if behind:
                    moments2(i - 1)
                if router:
                    choose_rows(i - 2)
                    keep_rows(i - 2, u)
            diagonal(0)
            scores(0, 0)
            masked(0, 0, 1)
            masked(0, 0, 0)
            negated_max(0, 0)
            scores(1, 1)
            steps(dve, attend)
            for part in (gate_sum, gate_first, gate_second):
                part(T - 1, (T - 1) % 2)

            dve.wait_ge(s_slot, T)
            dve.tensor_copy(tail_row[0:1, :], count[0:1, :]).then_inc(s_tail_in, 1)
            link, n = chain(dve, s_ds, base)
            cnt, til, cum, one, nxt = (small[0:1, k * E:(k + 1) * E] for k in range(5))
            link(dve.scalar_tensor_tensor(out=cnt, in0=iota_e[0:1, :], scalar=-float(REGION), in1=count[0:1, :], op0=ALU.mult, op1=ALU.add))
            link(dve.tensor_scalar(nxt.bitcast(I32), cnt, R / 2 - 0.5, 1.0 / R, ALU.add, ALU.mult))
            link(dve.tensor_copy(til, nxt.bitcast(I32)))
            link(dve.memset(one, 1.0))
            link(dve.tensor_tensor_scan(cum, one, til, 0.0, ALU.mult, ALU.add))
            link(dve.tensor_scalar(nxt, til, -float(R), float(REGION), ALU.mult, ALU.add))
            ended, jump = (tb[:, k * E * FT:(k + 1) * E * FT].rearrange("o (e t) -> o e t", e=E) for k in range(2))
            t_of = iota_t[:, :].rearrange("o (a t) -> o a t", a=1).broadcast_to([1, E, FT])
            cum_of = cum.rearrange("o (e a) -> o e a", a=1).broadcast_to([1, E, FT])
            nxt_of = nxt.rearrange("o (e a) -> o e a", a=1).broadcast_to([1, E, FT])
            link(dve.tensor_tensor(ended, t_of, cum_of, ALU.is_ge))
            link(dve.tensor_tensor(jump, ended, nxt_of, ALU.mult))
            ex, row, past = (tb[:, (2 * E + k) * FT:(2 * E + k + 1) * FT] for k in range(3))
            link(dve.tensor_reduce(ex, ended[:, 0:E - 1, :].rearrange("o e t -> o t e"), mybir.AxisListType.X, ALU.add))
            link(dve.tensor_reduce(row, jump[:, 0:E - 1, :].rearrange("o e t -> o t e"), mybir.AxisListType.X, ALU.add))
            dve.tensor_copy(table_e[0:1, :], ex).then_inc(s_te, 1)
            link(dve.scalar_tensor_tensor(out=row, in0=iota_t[:, :], scalar=float(R), in1=row, op0=ALU.mult, op1=ALU.add))
            link(dve.tensor_scalar(past, row, -1.0, count[0:1, E - 1:E], ALU.mult, ALU.add))
            link(dve.tensor_tensor(past, past, ended[:, E - 1, :], ALU.mult))
            link(dve.tensor_tensor(row, row, past, ALU.add))
            dve.wait_ge(s_te, 1)
            dve.tensor_copy(table_row[0:1, :], row).then_inc(s_tab, 1)
            for u in range(2):
                dve.wait_ge(s_sc[u], 32 * TO)

            def split_x(t):
                dve.wait_ge(s_xg, t + 1)
                if within(t, 1, FT):
                    dve.wait_ge(s_g1, 2 * t)
                dve.tensor_copy(x_hi[:, :], xg[:, :]).then_inc(s_xc, 1)
                dve.tensor_scalar(x_down[:, :], xg[:, :], 1.0 / LOSCALE, None, ALU.mult).then_inc(s_xc, 1)
                dve.wait_ge(s_xc, 2 * t + 2)
                dve.tensor_tensor(x_lo[:, :], xg[:, :], x_hi[:, :], ALU.subtract).then_inc(s_xh, 1)

            def split_h(t, u):
                dve.wait_ge(s_ge1, 2 * t + 2)
                if within(t, 2, FT):
                    dve.wait_ge(s_g2, t - 1)
                dve.tensor_copy(h_hi[u][:, :], hf[:, :]).then_inc(s_hc, 1)
                dve.wait_ge(s_hc, t + 1)
                dve.tensor_tensor(h_lo[u][:, :], hf[:, :], h_hi[u][:, :], ALU.subtract).then_inc(s_hh, 1)

            def result(t, u):
                e = dve.value_load(table_e[0:1, bass.ds(t, 1)], min_val=0, max_val=E - 1)
                dve.wait_ge(s_g2, t + 1)
                if within(t, 1, FT):
                    dve.wait_ge(s_ysc, 16 * S * t)
                for s in range(S):
                    dve.scalar_tensor_tensor(out=y_sb[:, s, :], in0=acc[s][:, D:2 * D], scalar=1.0 / LOSCALE,
                                             in1=b2_rep[:, bass.ds(e * D, D)], op0=ALU.mult, op1=ALU.add).then_inc(s_yc, 1)
                dve.wait_ge(s_yc, YA * t + S)
                for s in range(S):
                    dve.tensor_tensor(y_sb[:, s, :], acc[s][:, 0:D], y_sb[:, s, :], ALU.add).then_inc(s_yc, 1)
                dve.wait_ge(s_yc, YA * t + 2 * S)
                dve.wait_ge(s_yi, YI * t + YI)
                for s in range(S):
                    ins = dve.tensor_scalar(y_sb[:, s, :], y_sb[:, s, :], weight[u][:, s:s + 1], None, ALU.mult)
                ins.then_inc(s_y, 1)

            split_x(0)
            split_x(1)
            split_h(0, 0)
            dve.wait_ge(s_b2, 16)

            def pair(t):
                split_x(t + 1)
                split_h(t, 1)
                result(t - 1, 0)
                split_x(t + 2)
                split_h(t + 1, 0)
                result(t, 1)

            pair(1)
            with dve.Fori(1, FT // 2 - 1) as o:
                pair(2 * o + 1)
            split_x(FT - 1)
            split_h(FT - 2, 1)
            result(FT - 3, 0)
            split_h(FT - 1, 0)
            result(FT - 2, 1)
            result(FT - 1, 0)


_INS = ["x", "adj", "L0_gnn_W", "L0_gnn_a", "L0_ffn_Wr", "L0_ffn_br", "L0_ffn_ln_g", "L0_ffn_ln_b",
        "L0_ffn_W1", "L0_ffn_b1", "L0_ffn_W2", "L0_ffn_b2"]


def kernel(**inputs):
    import numpy as _np
    import concourse.bacc as _bacc
    from concourse import mybir as _mybir
    from concourse.bass_utils import run_bass_kernel_spmd as _run

    nc = _bacc.Bacc("TRN2", target_bir_lowering=False, num_devices=1)
    arrays, args = {}, []
    for name in _INS:
        a = _np.ascontiguousarray(inputs[name])
        arrays[f"in_{name}"] = a
        args.append(nc.dram_tensor(f"in_{name}", a.shape, _mybir.dt.from_np(a.dtype), kind="ExternalInput").ap())
    n, d = inputs["x"].shape
    args.append(nc.dram_tensor("out_0", (n + DUMP, d), _mybir.dt.float32, kind="ExternalOutput").ap())
    build(nc, *args)
    r = _run(nc, [arrays], core_ids=[0])
    return r.results[0]["out_0"][:n]
```
